# Optimizing a Trainium2 kernel written in Bass

```python
import numpy as np
import jax
import jax.numpy as jnp

def _softmax(x, axis=-1):
    return jax.nn.softmax(x, axis=axis)

def _gelu(x):
    return jax.nn.gelu(x, approximate=True)

def _silu(x):
    return jax.nn.silu(x)

def _sigmoid(x):
    return jax.nn.sigmoid(x)

def _layernorm(x, axis=-1, eps=1e-05):
    m = jnp.mean(x, axis=axis, keepdims=True)
    v = jnp.var(x, axis=axis, keepdims=True)
    return (x - m) / jnp.sqrt(v + eps)

def _scatter_add(tgt, idx, src, axis=0):
    return tgt.at[idx].add(src)

def _segment_sum(src, seg, n):
    return jax.ops.segment_sum(src, seg, n)
kernel_name = 'mk_gnn_preln_d2_gnn_r16_5e939a'

def setup_inputs(seed: int=0):
    np.random.seed(seed)
    _w = jnp.asarray

    def _rec_inputs():
        import jax
        import jax.numpy as jnp
        _gk = jax.random.key(seed)
        x = -0.0003713 + 1 * jax.random.normal(jax.random.fold_in(_gk, 1), (6250, 256), jnp.float32)
        _s = jax.random.randint(jax.random.fold_in(_gk, 2), (50000,), 0, 6250, jnp.int32)
        _d = jax.random.randint(jax.random.fold_in(_gk, 3), (50000,), 0, 6250, jnp.int32)
        _loop = jnp.arange(6250, dtype=jnp.int32)
        src = jnp.concatenate([_s, _d, _loop])
        dst = jnp.concatenate([_d, _s, _loop])
        _o = jnp.argsort(dst, stable=True)
        src = src[_o]
        dst = dst[_o]
        edge_type_8 = jax.random.randint(jax.random.fold_in(_gk, 13), (106250,), 0, 8, jnp.int32)
        return (x, src, dst, edge_type_8)
    x, src, dst, edge_type_8 = _rec_inputs()

    def _L0_gnn_setup():
        import jax, jax.numpy as jnp
        import numpy as np
        N, E, D, R, L = (3125, 15625, 256, 8, 3)
        key = jax.random.key(seed)
        k = jax.random.split(key, 7)
        scale = 1.0 / np.sqrt(D)
        x = jax.random.normal(k[0], (N, D), dtype=jnp.float32)
        edge_index = jax.random.randint(k[1], (2, E), 0, N, dtype=jnp.int64)
        edge_type = jax.random.randint(k[2], (E,), 0, R, dtype=jnp.int64)
        W_rel = jax.random.normal(k[3], (L, R, D, D), dtype=jnp.float32) * scale
        W_root = jax.random.normal(k[4], (L, D, D), dtype=jnp.float32) * scale
        bias = jax.random.normal(k[5], (L, D), dtype=jnp.float32) * 0.02
        return {'x': x, 'edge_index': edge_index, 'edge_type': edge_type, 'W_rel': W_rel, 'W_root': W_root, 'bias': bias}
    _L0_gnn_all = _L0_gnn_setup()
    _L0_gnn_in = {k: v for k, v in _L0_gnn_all.items() if k in ('W_rel', 'W_root', 'bias')}
    del _L0_gnn_all

    def _L1_gnn_setup():
        import jax, jax.numpy as jnp
        import numpy as np
        N_NODES = 6250
        N_EDGES = 200000
        IN_F = 256
        OUT_F = 256
        NEG_SLOPE = 0.2
        key = jax.random.key(seed)
        ks = jax.random.split(key, 8)
        x = jax.random.normal(ks[0], (N_NODES, IN_F), dtype=jnp.float32)
        Wv = jax.random.normal(ks[1], (IN_F, OUT_F), dtype=jnp.float32) / np.sqrt(IN_F)
        bv = jnp.zeros((OUT_F,), dtype=jnp.float32)
        wq = jax.random.normal(ks[2], (OUT_F,), dtype=jnp.float32) / np.sqrt(OUT_F)
        bq = jnp.zeros((), dtype=jnp.float32)
        wk = jax.random.normal(ks[3], (OUT_F,), dtype=jnp.float32) / np.sqrt(OUT_F)
        bk = jnp.zeros((), dtype=jnp.float32)
        src = jax.random.randint(ks[4], (N_EDGES,), 0, N_NODES, dtype=jnp.int32)
        dst = jax.random.randint(ks[5], (N_EDGES,), 0, N_NODES, dtype=jnp.int32)
        return {'x': x, 'Wv': Wv, 'bv': bv, 'wq': wq, 'bq': bq, 'wk': wk, 'bk': bk, 'src': src, 'dst': dst}
    _L1_gnn_all = _L1_gnn_setup()
    _L1_gnn_in = {k: v for k, v in _L1_gnn_all.items() if k in ('Wv', 'bv', 'wq', 'bq', 'wk', 'bk')}
    del _L1_gnn_all
    return {'x': x, 'src': src, 'dst': dst, 'edge_type_8': edge_type_8, 'L0_gnn_W_rel': _L0_gnn_in['W_rel'], 'L0_gnn_W_root': _L0_gnn_in['W_root'], 'L0_gnn_bias': _L0_gnn_in['bias'], 'L1_gnn_Wv': _L1_gnn_in['Wv'], 'L1_gnn_bv': _L1_gnn_in['bv'], 'L1_gnn_wq': _L1_gnn_in['wq'], 'L1_gnn_bq': _L1_gnn_in['bq'], 'L1_gnn_wk': _L1_gnn_in['wk'], 'L1_gnn_bk': _L1_gnn_in['bk']}

def reference(x, src, dst, edge_type_8, L0_gnn_W_rel, L0_gnn_W_root, L0_gnn_bias, L1_gnn_Wv, L1_gnn_bv, L1_gnn_wq, L1_gnn_bq, L1_gnn_wk, L1_gnn_bk):
    import jax
    import jax.numpy as jnp

    def _L0_gnn_ref(x, edge_index, edge_type, W_rel, W_root, bias):
        import jax, jax.numpy as jnp
        import numpy as np
        N, E, D, R, L = (3125, 15625, 256, 8, 3)
        src, dst = (edge_index[0], edge_index[1])
        n_layers = W_rel.shape[0]
        for l in range(n_layers):
            xr = jnp.einsum('nd,rde->rne', x, W_rel[l])
            msg = xr[edge_type, src]
            agg = jax.ops.segment_sum(msg, dst, num_segments=x.shape[0])
            x = jax.nn.relu(agg + x @ W_root[l] + bias[l])
        return x

    def _L1_gnn_ref(x, Wv, bv, wq, bq, wk, bk, src, dst):
        import jax, jax.numpy as jnp
        import numpy as np
        N_NODES = 6250
        N_EDGES = 200000
        IN_F = 256
        OUT_F = 256
        NEG_SLOPE = 0.2
        n = x.shape[0]
        h = x @ Wv + bv
        q = h @ wq + bq
        k = h @ wk + bk
        e = q[src] + k[dst]
        c = jnp.where(e > 0, e, NEG_SLOPE * e)
        m = jax.ops.segment_max(c, dst, num_segments=n)
        ex = jnp.exp(c - m[dst])
        s = jax.ops.segment_sum(ex, dst, num_segments=n)
        attn = ex / s[dst]
        msg = h[src] * attn[:, None]
        out = jax.ops.segment_sum(msg, dst, num_segments=n)
        return out
    edge_index = jnp.stack([src, dst])
    h = jnp.maximum(_layernorm(x, axis=-1), 0.0)
    x = x + _L0_gnn_ref(h, edge_index, edge_type_8, L0_gnn_W_rel, L0_gnn_W_root, L0_gnn_bias)
    h = jnp.maximum(_layernorm(x, axis=-1), 0.0)
    x = x + _L1_gnn_ref(h, L1_gnn_Wv, L1_gnn_bv, L1_gnn_wq, L1_gnn_bq, L1_gnn_wk, L1_gnn_bk, src, dst)
    return x

_drawn_inputs = setup_inputs


def setup_inputs(seed=0):
    import zlib

    import numpy as np

    out = dict(_drawn_inputs(seed))
    spreads = {'L1_gnn_bv': (0.0, 0.8)}
    factors = {'L0_gnn_bias': 8.0, 'L1_gnn_Wv': 4.965, 'L1_gnn_wq': 8.0, 'L1_gnn_wk': 8.0}
    for name, (base, spread) in spreads.items():
        noise = np.random.default_rng([zlib.crc32(name.encode()), seed]).standard_normal(out[name].shape)
        drawn = base * np.exp(spread * noise) if base else spread * noise
        out[name] = jnp.asarray(drawn.astype(out[name].dtype))
    for name, factor in factors.items():
        out[name] = (out[name] * factor).astype(out[name].dtype)
    return out
```

```python
import numpy as np
import concourse.bass as bass
from concourse import mybir
from contextlib import ExitStack

F32 = mybir.dt.float32
I32 = mybir.dt.int32
ALU = mybir.AluOpType
ACT = mybir.ActivationFunctionType
AX = mybir.AxisListType

P = 128
EPS = 1e-5
SLOPE = 0.2
FAR = 1e30
LEAST_MAX = -1e29


def gnn_program(nc, x, src, dst, etype, w_rel, w_root, bias, wv, bv, wq, bq, wk, bk, out):
    N, D = x.shape
    E = src.shape[0]
    L, R = w_rel.shape[0], w_rel.shape[1]
    K = D // P
    NT = (N + P - 1) // P
    LAST = N - (NT - 1) * P
    PAIRS = NT // 2
    assert NT % 2 == 1 and D == K * P and R % 2 == 0
    USES = [PAIRS + 1, PAIRS]
    MEAN = -(-E * P // N)
    CHUNK = 3
    CHUNKS = -(-(MEAN + P) // (P * CHUNK))
    assert CHUNKS % 2 == 0
    SLOTS = CHUNK * CHUNKS
    BLOCK = SLOTS * P
    MAXB = -(-E // BLOCK) + 1
    EROWS = 125
    ECOLS = E // EROWS
    assert E == EROWS * ECOLS
    PADROWS = -(-MAXB * BLOCK // (EROWS * ECOLS))
    EPAD = E * (1 + PADROWS)
    G16 = 16
    GCOLS = -(-E // (P * G16))
    NGROUPS = P * GCOLS
    TROWS = NT * P * R
    HROW = D + 4
    TW = R * D
    CW = CHUNK * P

    tables = [nc.dram_tensor(f"table{l}", (TROWS, D), F32, kind="Internal").ap() for l in range(L)]
    tables_by_node = [t.rearrange("(n r) d -> n (r d)", r=R) for t in tables]
    h_table = nc.dram_tensor("h_table", (NT * P, HROW), F32, kind="Internal").ap()
    code_dram = nc.dram_tensor("code_dram", (EPAD,), I32, kind="Internal").ap()
    dst_dram = nc.dram_tensor("dst_dram", (EPAD,), F32, kind="Internal").ap()

    ctx = ExitStack()
    with ctx:
        def sb(name, shape, dt=F32):
            return ctx.enter_context(nc.sbuf_tensor(name, shape, dt))

        def sem(name):
            return ctx.enter_context(nc.semaphore(name))

        def sems(name, n):
            return [sem(f"{name}{k}") for k in range(n)]

        root = sb("root", [P, NT, D])
        gathered = sb("gathered", [P, 2, SLOTS, HROW])
        masks = sb("masks", [P, 2, SLOTS, P])
        weights = sb("weights", [P, K, (R + 1) * D])
        stage = sb("stage", [P, 2, TW])
        code = sb("code", [P, NT + 1, SLOTS], I32)
        local = sb("local", [P, NT + 1, SLOTS])
        index = [sb(f"index{b}", [P, SLOTS], I32) for b in range(2)]
        x_tile = sb("x_tile", [P, 2, D])
        z = sb("z", [P, 2, D])
        xT = sb("xT", [P, 2, K, P])
        bias_row = sb("bias_row", [P, D])
        wv_sb = sb("wv_sb", [P, K, D])
        bv_row = sb("bv_row", [P, D])
        wq_row = sb("wq_row", [P, D])
        wk_row = sb("wk_row", [P, D])
        bqk = sb("bqk", [P, 2])
        h_row = sb("h_row", [P, 2, HROW])
        product = sb("product", [P, D])
        summed = sb("summed", [P, D])
        key = sb("key", [P, NT + 1])
        far_max = sb("far_max", [P, NT + 1])
        far_sum = sb("far_sum", [P, NT + 1])
        all_sum = sb("all_sum", [P, NT + 1])
        stats = sb("stats", [P, 6])
        mean_var = sb("mean_var", [P, 2])
        std = sb("std", [P, 1])
        rstd = sb("rstd", [P, 1])
        eps = sb("eps", [P, 1])
        chunk_max = sb("chunk_max", [P, CHUNKS])
        top = sb("top", [P, 1])
        neg_max = sb("neg_max", [P, 1])
        chunk_sum = sb("chunk_sum", [P, CHUNKS])
        denom = sb("denom", [P, 3])
        ident = sb("ident", [P, P])
        node_row = sb("node_row", [P, P])
        tile_base = sb("tile_base", [P, NT + 1])
        starts = sb("starts", [1, NT], I32)
        extra_blocks = sb("extra_blocks", [1, 1], I32)
        far_code = sb("far_code", [P, SLOTS], I32)
        far_dst = sb("far_dst", [P, SLOTS])
        far_local = sb("far_local", [P, SLOTS])
        scores = weights[:, 0, 0:SLOTS * P]
        attn = weights[:, 1, 0:SLOTS * P]
        prep = gathered[:, :, :, :].rearrange("p b s d -> p (b s d)")

        at = [0]

        def room(rows, cols, dt=F32):
            part = prep[0:rows, at[0]:at[0] + cols]
            at[0] += cols
            return part if dt == F32 else part.bitcast(dt)

        src_i, type_i, dst_i = (room(EROWS, ECOLS, I32) for _ in range(3))
        dst_f = room(EROWS, ECOLS)
        at[0] = 0
        groups = room(P, GCOLS * G16)
        least, most = room(P, GCOLS), room(P, GCOLS)
        from_end, from_start = room(P, GCOLS), room(P, GCOLS)
        last_node = room(P, NT)
        meets = room(P, NT * GCOLS).rearrange("p (t g) -> p t g", g=GCOLS)
        other = room(P, NT * GCOLS).rearrange("p (t g) -> p t g", g=GCOLS)
        ends, over_all = room(P, 2 * NT), room(P, 2 * NT)
        start_f, length, top_length = room(1, NT), room(1, NT), room(1, 1)
        block_edges, over = room(1, 64), room(1, 64)
        assert MAXB <= 64 and at[0] <= 2 * SLOTS * HROW
        BOUNDS_STEPS = 10
        CONSTS = 11

        sum_ps = [ctx.enter_context(nc.psum_tensor(f"sum_ps{b}", [P, 512], F32)) for b in range(2)]
        turn_ps = ctx.enter_context(nc.psum_tensor("turn_ps", [P, K, P], F32))
        NB = R // 2 + 1
        bank = [ctx.enter_context(nc.psum_tensor(f"bank{q}", [P, 512], F32)) for q in range(NB)]
        score_ps, attn_ps = bank[0:2], bank[2:4]

        consts_ready = sem("consts_ready")
        prep_step = sem("prep_step")
        prep_dma = sem("prep_dma")
        groups_loaded, numbers_ready = sem("groups_loaded"), sem("numbers_ready")
        bounds_step = sem("bounds_step")
        ends_reduced = sem("ends_reduced")
        starts_ready = sem("starts_ready")
        blocks_loaded = sem("blocks_loaded")
        blocks_local = sem("blocks_local")
        params_loaded = sem("params_loaded")
        weights_loaded = sem("weights_loaded")
        x_loaded = sems("x_loaded", 2)
        stats_ready, mv_ready, rstd_ready = sem("stats_ready"), sem("mv_ready"), sem("rstd_ready")
        std_ready = sem("std_ready")
        z_ready = sems("z_ready", 2)
        turned = sems("turned", 2)
        xT_ready = sems("xT_ready", 2)
        transformed = sems("transformed", 2)
        evacuated = sems("evacuated", NB)
        stored = sems("stored", 2)
        index_ready = sems("index_ready", 2)
        arrived = [sems(f"arrived{b}_", CHUNKS) for b in range(2)]
        mask_ready = sems("mask_ready", 2)
        aggregated = [sems(f"aggregated{b}_", CHUNKS) for b in range(2)]
        summed_ready, residual_ready = sem("summed_ready"), sem("residual_ready")
        h_ready = sems("h_ready", 2)
        h_biased = sems("h_biased", 2)
        dot_ready = sem("dot_ready")
        qk_ready = sems("qk_ready", 2)
        h_stored = sems("h_stored", 2)
        code_shifted = sem("code_shifted")
        masked = sems("masked", 2)
        score_turned = sem("score_turned")
        scored = sems("scored", CHUNKS)
        leaked = sem("leaked")
        max_done = sem("max_done")
        top_ready = sem("top_ready")
        neg_max_ready = sem("neg_max_ready")
        exp_ready = sem("exp_ready")
        attn_turned = sems("attn_turned", CHUNKS)
        attn_ready = sems("attn_ready", CHUNKS)
        denom_step = sem("denom_step")
        out_ready = sems("out_ready", 2)
        out_stored = sems("out_stored", 2)
        far_loaded, far_index, far_arrived, far_localised = (
            sem("far_loaded"), sem("far_index"), sem("far_arrived"), sem("far_localised"))
        far_mask, far_aggregated, far_done = sem("far_mask"), sem("far_aggregated"), sem("far_done")
        f_loaded, f_index, f_arrived, f_localised = (
            sem("f_loaded"), sem("f_index"), sem("f_arrived"), sem("f_localised"))
        f_mask, f_masked, f_turned, f_scored, f_done = (
            sem("f_mask"), sem("f_masked"), sem("f_turned"), sem("f_scored"), sem("f_done"))
        f_top, f_neg, f_exp, f_inverse = sem("f_top"), sem("f_neg"), sem("f_exp"), sem("f_inverse")
        f_back, f_attn, f_aggregated = sem("f_back"), sem("f_attn"), sem("f_aggregated")
        f_sums, f_leaked = sem("f_sums"), sem("f_leaked")

        def settle(eng, *values):
            for value in values:
                if not isinstance(value, int):
                    eng.lower_val(value)
            eng.wait_ge(consts_ready, CONSTS)

        def over_tiles(eng, body):
            with eng.Fori(0, PAIRS) as j:
                body(2 * j, j, 0)
                body(2 * j + 1, j, 1)
            body(NT - 1, PAIRS, 0)

        def slot_columns(t, b, c):
            return t[:, b, CHUNK * c:CHUNK * (c + 1), :]

        def columns(t, c):
            return t[:, CW * c:CW * (c + 1)]

        loaded_extra = {}

        def load_extra_blocks(eng):
            eng.wait_ge(blocks_local, 1)
            loaded_extra[eng.engine] = eng.value_load(extra_blocks[0:1, 0:1], min_val=0, max_val=MAXB)

        def extra(eng):
            return loaded_extra[eng.engine]

        def further(eng, body):
            with eng.Fori(0, extra(eng)) as k:
                with eng.Fori(0, NT) as i:
                    body(k, i)

        def attention_phases(eng, body):
            n = extra(eng)
            with eng.Fori(0, NT) as i:
                body("max", -1, i, i, 0)
            further(eng, lambda k, i: body("max", k, i, (1 + k) * NT + i, 0))
            with eng.Fori(0, NT) as i:
                body("first sum", -1, i, (1 + n) * NT + i, i)
            further(eng, lambda k, i: body("sum", k, i, (2 + n + k) * NT + i, (1 + k) * NT + i))
            further(eng, lambda k, i: body("apply", k, i, (2 + n + n + k) * NT + i, (1 + n + k) * NT + i))

        block = ctx.enter_context(nc.Block())

        @block.gpsimd
        def _(pool):
            pool.iota(node_row[:, :], [[1, P]], base=0, channel_multiplier=0,
                      allow_small_or_imprecise_dtypes=True).then_inc(consts_ready, 1)
            pool.iota(tile_base[:, :], [[P, NT + 1]], base=0, channel_multiplier=0,
                      allow_small_or_imprecise_dtypes=True).then_inc(consts_ready, 1)
            pool.memset(ident[:, :], 0.0).then_inc(prep_step, 1)
            steps = [1]

            def step(instruction):
                steps[0] += 1
                instruction.then_inc(prep_step, 1)
                pool.wait_ge(prep_step, steps[0])

            pool.wait_ge(prep_step, 1)
            pool.affine_select(out=ident[:, :], in_=ident[:, :], compare_op=ALU.not_equal, fill=1.0, base=0,
                               pattern=[[-1, P]], channel_multiplier=1).then_inc(consts_ready, 1)
            pool.memset(far_max[:, :], LEAST_MAX).then_inc(consts_ready, 1)
            pool.memset(far_sum[:, :], 1e-30).then_inc(consts_ready, 1)
            pool.memset(eps[:, :], EPS).then_inc(consts_ready, 1)
            pool.memset(all_sum[:, :], 0.0).then_inc(consts_ready, 1)
            pool.memset(x_tile[:, :, :], 0.0).then_inc(consts_ready, 1)
            pool.memset(h_row[:, :, :], 0.0).then_inc(consts_ready, 1)
            pool.memset(code[:, NT, :], 0).then_inc(consts_ready, 1)
            pool.memset(index[1][:, :], 0).then_inc(consts_ready, 1)

            for to, of in ((src_i, src), (type_i, etype), (dst_i, dst)):
                pool.dma_start(to, of.rearrange("(p c) -> p c", p=EROWS)).then_inc(prep_dma, 16)
            pool.wait_ge(prep_dma, 48)
            step(pool.tensor_copy(dst_f, dst_i))
            step(pool.tensor_scalar(src_i, src_i, float(R), None, ALU.mult))
            step(pool.tensor_tensor(src_i, src_i, type_i, ALU.add))
            pool.dma_start(dst_dram[0:E].rearrange("(p c) -> p c", p=EROWS), dst_f).then_inc(prep_dma, 16)
            pool.dma_start(code_dram[0:E].rearrange("(p c) -> p c", p=EROWS), src_i).then_inc(prep_dma, 16)
            step(pool.memset(type_i, 0))
            step(pool.memset(dst_i.bitcast(F32), 1e6))
            for k in range(1, 1 + PADROWS):
                pool.dma_start(code_dram[k * E:(k + 1) * E].rearrange("(p c) -> p c", p=EROWS),
                               type_i).then_inc(prep_dma, 16)
                pool.dma_start(dst_dram[k * E:(k + 1) * E].rearrange("(p c) -> p c", p=EROWS),
                               dst_i.bitcast(F32)).then_inc(prep_dma, 16)
            done = 48 + 32 + 32 * PADROWS
            pool.wait_ge(prep_dma, done)

            pool.dma_start(groups, dst_dram[0:NGROUPS * G16].rearrange("(p c) -> p c", p=P)).then_inc(groups_loaded, 16)
            step(pool.iota(from_end, [[-1, GCOLS]], base=NGROUPS, channel_multiplier=-GCOLS,
                           allow_small_or_imprecise_dtypes=True))
            step(pool.iota(from_start, [[1, GCOLS]], base=1, channel_multiplier=GCOLS,
                           allow_small_or_imprecise_dtypes=True))
            pool.iota(block_edges, [[BLOCK, 64]], base=BLOCK, channel_multiplier=0,
                      allow_small_or_imprecise_dtypes=True).then_inc(numbers_ready, 1)
            pool.wait_ge(bounds_step, BOUNDS_STEPS)
            pool.partition_all_reduce(over_all, ends, P, bass.bass_isa.ReduceOp.max).then_inc(ends_reduced, 1)
            pool.wait_ge(starts_ready, 2)

            with pool.Fori(0, NT) as i:
                start = pool.value_load(starts[0:1, bass.ds(i, 1)], min_val=0, max_val=E)
                pool.dma_start(code[:, i, :], code_dram[bass.ds(start, BLOCK)].rearrange("(p s) -> p s", p=P)
                               ).then_inc(blocks_loaded, 16)
                pool.dma_start(local[:, i, :], dst_dram[bass.ds(start, BLOCK)].rearrange("(p s) -> p s", p=P)
                               ).then_inc(blocks_loaded, 16)
            pool.wait_ge(blocks_loaded, 32 * NT)
            pool.tensor_tensor(local[:, 0:NT, :], local[:, 0:NT, :],
                               tile_base[:, 0:NT].unsqueeze(2).to_broadcast([P, NT, SLOTS]), ALU.subtract
                               ).then_inc(blocks_local, 1)
            load_extra_blocks(pool)

            def gather_tile(l, j, b, table, width):
                use = l * USES[b] + j
                settle(pool, l * (PAIRS + 1) + j + 1, use)
                pool.wait_ge(index_ready[b], l * (PAIRS + 1) + j + 1)
                for c in range(CHUNKS):
                    settle(pool, use)
                    pool.wait_ge(aggregated[b][c], use)
                    for s in range(CHUNK * c, CHUNK * (c + 1)):
                        pool.indirect_dma_start(
                            gathered[:, b, s, 0:width], None, table,
                            bass.IndirectOffsetOnAxis(ap=index[b][:, s:s + 1], axis=0)).then_inc(arrived[b][c], 16)

            def gather_pass(l, table, width):
                over_tiles(pool, lambda i, j, b: gather_tile(l, j, b, table, width))

            def wait_tables(l):
                settle(pool, *(16 * USES[b] * (l + 1) for b in range(2)))
                for b in range(2):
                    pool.wait_ge(stored[b], 16 * USES[b] * (l + 1))

            def far_gather(x_done, wait_index, arrives, table, width):
                settle(pool, x_done + 1)
                pool.wait_ge(wait_index, x_done + 1)
                for s in range(SLOTS):
                    pool.indirect_dma_start(
                        gathered[:, 0, s, 0:width], None, table,
                        bass.IndirectOffsetOnAxis(ap=index[0][:, s:s + 1], axis=0)).then_inc(arrives, 16)

            def conv_layer(l):
                wait_tables(l)
                nb = extra(pool)
                with pool.If(nb > 0):
                    further(pool, lambda k, i: far_gather((l * nb + k) * NT + i, far_index, far_arrived,
                                                          tables[l], D))
                    pool.wait_ge(far_done, (l + 1) * nb * NT)
                gather_pass(l, tables[l], D)

            for l in range(L):
                conv_layer(l)

            for b in range(2):
                pool.wait_ge(h_stored[b], 16 * USES[b])
            nb = extra(pool)
            with pool.If(nb > 0):
                attention_phases(pool, lambda phase, k, i, number, passed: far_gather(
                    number, f_index, f_arrived, h_table, HROW))
                pool.wait_ge(f_done, (2 + nb + nb + nb) * NT)
            gather_pass(L, h_table, HROW)

        @block.sync
        def _(sp):
            def load_weights(l):
                for k in range(K):
                    sp.dma_start(weights[:, k, 0:R * D].rearrange("p (r e) -> p r e", r=R),
                                 w_rel[l, :, k * P:(k + 1) * P, :].rearrange("r p e -> p r e")
                                 ).then_inc(weights_loaded, 16)
                    sp.dma_start(weights[:, k, R * D:(R + 1) * D], w_root[l, k * P:(k + 1) * P, :]
                                 ).then_inc(weights_loaded, 16)
                sp.dma_start(bias_row[:, :], bias[l:l + 1, :].to_broadcast([P, D])).then_inc(weights_loaded, 16)

            def load_x(i, use, b, last=False):
                rows = LAST if last else P
                sp.wait_ge(z_ready[b], use)
                base = (NT - 1) * P if last else i * P
                sp.dma_start(x_tile[0:rows, b, :], x[bass.ds(base, rows), :]).then_inc(x_loaded[b], 16)

            def store_table(l, i, use, b):
                for q in range(R // 2):
                    sp.wait_ge(evacuated[q], NT * l + i + 1)
                sp.dma_start(tables_by_node[l][bass.ds(i * P, P), :], stage[:, b, :]
                             ).then_inc(stored[b], 16)

            sp.wait_ge(consts_ready, CONSTS)
            load_x(0, 0, 0)
            load_weights(0)
            for row, of in ((bv_row, bv), (wq_row, wq), (wk_row, wk)):
                sp.dma_start(row[:, :], of.unsqueeze(0).to_broadcast([P, D])).then_inc(params_loaded, 16)
            for k, of in enumerate((bq, bk)):
                sp.dma_start(bqk[:, k:k + 1], of.unsqueeze(0).to_broadcast([P, 1])).then_inc(params_loaded, 16)
            for k in range(K):
                sp.dma_start(wv_sb[:, k, :], wv[k * P:(k + 1) * P, :]).then_inc(params_loaded, 16)

            with sp.Fori(0, PAIRS - 1) as j:
                load_x(2 * j + 1, j, 1)
                store_table(0, 2 * j, j, 0)
                load_x(2 * j + 2, j + 1, 0)
                store_table(0, 2 * j + 1, j, 1)
            load_x(NT - 2, PAIRS - 1, 1)
            store_table(0, NT - 3, PAIRS - 1, 0)
            load_x(NT - 1, PAIRS, 0, last=True)
            store_table(0, NT - 2, PAIRS - 1, 1)
            store_table(0, NT - 1, PAIRS, 0)
            load_extra_blocks(sp)
            nb = extra(sp)

            def far_load(number, i, k, done, loads):
                sp.wait_ge(done, number)
                start = sp.value_load(starts[0:1, bass.ds(i, 1)], min_val=0, max_val=E)
                at = start + (k + 1) * BLOCK
                sp.dma_start(far_code[:, :], code_dram[bass.ds(at, BLOCK)].rearrange("(p s) -> p s", p=P)
                             ).then_inc(loads, 16)
                sp.dma_start(far_dst[:, :], dst_dram[bass.ds(at, BLOCK)].rearrange("(p s) -> p s", p=P)
                             ).then_inc(loads, 16)

            def far_conv(l):
                with sp.If(nb > 0):
                    further(sp, lambda k, i: far_load((l * nb + k) * NT + i, i, k, far_done, far_loaded))

            for l in range(L - 1):
                for q in range(NB):
                    sp.wait_ge(evacuated[q], NT * (l + 1))
                load_weights(l + 1)
                far_conv(l)
                over_tiles(sp, lambda i, j, b: store_table(l + 1, i, (l + 1) * USES[b] + j, b))

            far_conv(L - 1)

            def layer_norm_tile(i, j, b, last=False):
                load_x(i, L * USES[b] + j, b, last)

            def store_h(i, j, b):
                sp.wait_ge(qk_ready[b], 2 * (j + 1))
                sp.dma_start(h_table[bass.ds(i * P, P), :], h_row[:, b, :]).then_inc(h_stored[b], 16)

            layer_norm_tile(0, 0, 0)
            with sp.Fori(0, PAIRS - 1) as j:
                layer_norm_tile(2 * j + 1, j, 1)
                store_h(2 * j, j, 0)
                layer_norm_tile(2 * j + 2, j + 1, 0)
                store_h(2 * j + 1, j, 1)
            layer_norm_tile(NT - 2, PAIRS - 1, 1)
            store_h(NT - 3, PAIRS - 1, 0)
            layer_norm_tile(NT - 1, PAIRS, 0, last=True)
            store_h(NT - 2, PAIRS - 1, 1)
            store_h(NT - 1, PAIRS, 0)

            with sp.If(nb > 0):
                attention_phases(sp, lambda phase, k, i, number, passed: far_load(number, i, k, f_done, f_loaded))

            def store_out(i, j, b, last=False):
                sp.wait_ge(out_ready[b], j + 1)
                rows = LAST if last else P
                base = (NT - 1) * P if last else i * P
                sp.dma_start(out[bass.ds(base, rows), :], z[0:rows, b, :]).then_inc(out_stored[b], 16)

            with sp.Fori(0, PAIRS) as j:
                store_out(2 * j, j, 0)
                store_out(2 * j + 1, j, 1)
            store_out(NT - 1, PAIRS, 0, last=True)
            for b in range(2):
                sp.wait_ge(out_stored[b], 16 * USES[b])

        @block.vector
        def _(dve):
            dve.wait_ge(consts_ready, CONSTS)

            def statistics(of, t):
                nc.vector.bn_stats(stats[:, :], of).then_inc(stats_ready, 1)
                settle(dve, t + 1)
                dve.wait_ge(stats_ready, t + 1)
                nc.vector.bn_aggr(mean_var[:, :], stats[:, :]).then_inc(mv_ready, 1)
                dve.wait_ge(std_ready, t + 1)
                nc.vector.reciprocal(rstd[:, :], std[:, :]).then_inc(rstd_ready, 1)
                dve.wait_ge(mv_ready, t + 1)
                dve.wait_ge(rstd_ready, t + 1)

            def normalise(of, use, b):
                dve.wait_ge(turned[b], use)
                nc.vector.tensor_scalar(z[:, b, :], of, mean_var[:, 0:1], rstd[:, 0:1], ALU.subtract, ALU.mult
                                        ).then_inc(z_ready[b], 1)

            def evacuate(i, use, b):
                q = R // 2 - 1
                dve.wait_ge(transformed[b], NB * use + q + 1)
                dve.wait_ge(stored[b], 16 * use)
                nc.vector.tensor_copy(stage[:, b, 512 * q:512 * (q + 1)], bank[q][:, :]).then_inc(evacuated[q], 1)
                dve.wait_ge(transformed[b], NB * use + NB)
                nc.vector.tensor_tensor(root[:, i, :], bank[NB - 1][:, 0:D], bias_row[:, :], ALU.add
                                        ).then_inc(evacuated[NB - 1], 1)

            def first_norm(i, j, b):
                dve.wait_ge(x_loaded[b], 16 * (j + 1))
                statistics(x_tile[:, b, :], i)
                normalise(x_tile[:, b, :], j, b)

            bounds = [0]

            def step(instruction):
                bounds[0] += 1
                instruction.then_inc(bounds_step, 1)
                dve.wait_ge(bounds_step, bounds[0])

            full_g = [P, NT, GCOLS]

            def per_group(a):
                return a.unsqueeze(1).to_broadcast(full_g)

            def per_tile(a):
                return a.unsqueeze(2).to_broadcast(full_g)

            def group_ranges():
                dve.wait_ge(groups_loaded, 16)
                dve.wait_ge(numbers_ready, 1)
                grouped = groups.rearrange("p (g e) -> p g e", e=G16)
                step(nc.vector.tensor_reduce(least, grouped, AX.X, ALU.min))
                step(nc.vector.tensor_reduce(most, grouped, AX.X, ALU.max))
                step(nc.vector.tensor_scalar(last_node, tile_base[:, 0:NT], float(P - 1), None, ALU.add))

            def reach_start():
                step(nc.vector.tensor_tensor(meets, per_group(most), per_tile(tile_base[:, 0:NT]), ALU.is_ge))
                step(nc.vector.tensor_tensor(other, per_group(least), per_tile(last_node), ALU.is_le))

            def both():
                step(nc.vector.tensor_tensor(meets, meets, other, ALU.mult))

            def end_of(k, number):
                step(nc.vector.tensor_tensor(other, meets, per_group(number), ALU.mult))
                step(nc.vector.tensor_reduce(ends[:, k * NT:(k + 1) * NT], other, AX.X, ALU.max))

            def block_starts():
                assert bounds[0] == BOUNDS_STEPS
                dve.wait_ge(ends_reduced, 1)
                step(nc.vector.tensor_scalar(start_f, over_all[0:1, 0:NT], -float(G16), float(G16 * NGROUPS),
                                             ALU.mult, ALU.add))
                step(nc.vector.tensor_scalar(start_f, start_f, float(E), None, ALU.min))
                step(nc.vector.scalar_tensor_tensor(length, over_all[0:1, NT:2 * NT], float(G16), start_f,
                                                    ALU.mult, ALU.subtract))
                nc.vector.tensor_copy(starts[:, :], start_f).then_inc(starts_ready, 1)
                step(nc.vector.tensor_reduce(top_length, length, AX.X, ALU.max))
                step(nc.vector.tensor_tensor(over, block_edges, top_length.to_broadcast([1, 64]), ALU.is_lt))
                step(nc.vector.tensor_reduce(top_length, over, AX.X, ALU.add))
                nc.vector.tensor_copy(extra_blocks[:, :], top_length).then_inc(starts_ready, 1)

            def before_layers(first, end):
                with dve.Fori(first, end) as j:
                    first_norm(2 * j + 1, j, 1)
                    evacuate(2 * j, j, 0)
                    first_norm(2 * j + 2, j + 1, 0)
                    evacuate(2 * j + 1, j, 1)

            first_norm(0, 0, 0)
            dve.wait_ge(weights_loaded, 16 * (2 * K + 1))
            parts = [group_ranges, reach_start, both, lambda: end_of(0, from_end), lambda: end_of(1, from_start),
                     block_starts]
            before_layers(0, 4)
            for k, part in enumerate(parts):
                part()
                before_layers(4 + 2 * k, 6 + 2 * k)
            before_layers(4 + 2 * len(parts), PAIRS)
            evacuate(NT - 1, PAIRS, 0)
            load_extra_blocks(dve)
            nb = extra(dve)

            full = [P, SLOTS, P]

            def list_rows(i, b):
                nc.vector.tensor_copy(index[b][:, :], code[:, i, :]).then_inc(index_ready[b], 1)

            def build_mask(i, b, compare):
                nc.vector.tensor_tensor(masks[:, b, :, :], node_row[:, :].unsqueeze(1).to_broadcast(full),
                                        local[:, i, :].unsqueeze(2).to_broadcast(full), compare
                                        ).then_inc(mask_ready[b], 1)

            def far_conv_block(number, i):
                dve.wait_ge(far_loaded, 32 * (number + 1))
                nc.vector.tensor_copy(index[0][:, :], far_code[:, :]).then_inc(far_index, 1)
                nc.vector.tensor_scalar(far_local[:, :], far_dst[:, :], tile_base[:, bass.ds(i, 1)], None, ALU.subtract
                                        ).then_inc(far_localised, 1)
                dve.wait_ge(far_localised, number + 1)
                nc.vector.tensor_tensor(masks[:, 0, :, :], node_row[:, :].unsqueeze(1).to_broadcast(full),
                                        far_local[:, :].unsqueeze(2).to_broadcast(full), ALU.is_equal
                                        ).then_inc(far_mask, 1)
                dve.wait_ge(far_aggregated, number + 1)
                nc.vector.tensor_tensor(root[:, i, :], sum_ps[0][:, 0:D], root[:, i, :], ALU.add
                                        ).then_inc(far_done, 1)
                dve.wait_ge(far_done, number + 1)

            def conv_head(l):
                settle(dve, NT * (l + 1))
                dve.wait_ge(evacuated[NB - 1], NT * (l + 1))
                with dve.If(nb > 0):
                    further(dve, lambda k, i: far_conv_block((l * nb + k) * NT + i, i))
                list_rows(0, 0)
                list_rows(1, 1)
                build_mask(0, 0, ALU.is_equal)

            def conv_tile(l, i, j, b, last):
                use = l * USES[b] + j
                if not last:
                    build_mask(i + 1, 1 - b, ALU.is_equal)
                dve.wait_ge(aggregated[b][CHUNKS - 1], use + 1)
                if not last:
                    list_rows(i + 2, b)

            def to_next_layer(l, i, j, b, last=False):
                conv_tile(l, i, j, b, last)
                use = (l + 1) * USES[b] + j
                dve.wait_ge(turned[b], use)
                nc.vector.tensor_tensor(z[:, b, :], sum_ps[b][:, 0:D], root[:, i, :], ALU.add
                                        ).then_inc(z_ready[b], 1)
                evacuate(i, use, b)

            for l in range(L - 1):
                conv_head(l)
                settle(dve, 16 * (2 * K + 1) * (l + 2))
                dve.wait_ge(weights_loaded, 16 * (2 * K + 1) * (l + 2))
                with dve.Fori(0, PAIRS) as j:
                    to_next_layer(l, 2 * j, j, 0)
                    to_next_layer(l, 2 * j + 1, j, 1)
                to_next_layer(l, NT - 1, PAIRS, 0, last=True)

            conv_head(L - 1)
            dve.wait_ge(params_loaded, 16 * (5 + K))

            def to_attention(i, j, b, last=False):
                conv_tile(L - 1, i, j, b, last)
                nc.vector.tensor_tensor(summed[:, :], sum_ps[b][:, 0:D], root[:, i, :], ALU.add
                                        ).then_inc(summed_ready, 1)
                dve.wait_ge(summed_ready, i + 1)
                dve.wait_ge(x_loaded[b], 16 * (USES[b] + j + 1))
                nc.vector.scalar_tensor_tensor(root[:, i, :], summed[:, :], 0.0, x_tile[:, b, :], ALU.max, ALU.add
                                               ).then_inc(residual_ready, 1)
                settle(dve, i + 1)
                dve.wait_ge(residual_ready, i + 1)
                statistics(root[:, i, :], NT + i)
                normalise(root[:, i, :], L * USES[b] + j, b)
                dve.wait_ge(h_ready[b], j + 1)
                dve.wait_ge(h_stored[b], 16 * j)
                nc.vector.tensor_tensor(h_row[:, b, 0:D], bank[b][:, 0:D], bv_row[:, :], ALU.add
                                        ).then_inc(h_biased[b], 1)
                dve.wait_ge(h_biased[b], j + 1)
                for k, row in enumerate((wq_row, wk_row)):
                    nc.vector.scalar_tensor_tensor(product[:, :], h_row[:, b, 0:D], 1.0, row[:, :], ALU.mult, ALU.mult,
                                                   accum_out=denom[:, k:k + 1]).then_inc(dot_ready, 1)
                    dve.wait_ge(dot_ready, 2 * i + k + 1)
                nc.vector.tensor_scalar(h_row[:, b, D:D + 1], denom[:, 0:1], bqk[:, 0:1], None, ALU.add
                                        ).then_inc(qk_ready[b], 1)
                nc.vector.tensor_scalar(key[:, bass.ds(i, 1)], denom[:, 1:2], bqk[:, 1:2], None, ALU.add
                                        ).then_inc(qk_ready[b], 1)

            with dve.Fori(0, PAIRS) as j:
                to_attention(2 * j, j, 0)
                to_attention(2 * j + 1, j, 1)
            to_attention(NT - 1, PAIRS, 0, last=True)

            for b in range(2):
                dve.wait_ge(turned[b], (L + 1) * USES[b])
            nc.vector.tensor_scalar(code[:, :, :], code[:, :, :], R.bit_length() - 1, None, ALU.arith_shift_right
                                    ).then_inc(code_shifted, 1)
            dve.wait_ge(code_shifted, 1)

            def lower_others(b, s0, s1):
                return nc.vector.scalar_tensor_tensor(
                    masks[:, b, s0:s1, :], masks[:, b, s0:s1, :], -FAR,
                    gathered[:, b, s0:s1, D:D + 1].to_broadcast([P, s1 - s0, P]), ALU.mult, ALU.add)

            def leaky(part):
                return nc.vector.scalar_tensor_tensor(part, part, SLOPE, part, ALU.mult, ALU.max)

            def far_attention_block(phase, k, i, number, passed):
                dve.wait_ge(f_loaded, 32 * (number + 1))
                nc.vector.tensor_scalar(index[0][:, :], far_code[:, :], R.bit_length() - 1, None,
                                        ALU.arith_shift_right).then_inc(f_index, 1)
                nc.vector.tensor_scalar(far_local[:, :], far_dst[:, :], tile_base[:, bass.ds(i, 1)], None, ALU.subtract
                                        ).then_inc(f_localised, 1)
                dve.wait_ge(f_localised, number + 1)
                nc.vector.tensor_tensor(masks[:, 0, :, :], node_row[:, :].unsqueeze(1).to_broadcast(full),
                                        far_local[:, :].unsqueeze(2).to_broadcast(full), ALU.not_equal
                                        ).then_inc(f_mask, 1)
                dve.wait_ge(f_mask, number + 1)
                dve.wait_ge(f_arrived, 16 * SLOTS * (number + 1))
                lower_others(0, 0, SLOTS).then_inc(f_masked, 1)
                dve.wait_ge(f_scored, CHUNKS * (number + 1))
                leaky(scores).then_inc(f_leaked, 1)
                dve.wait_ge(f_leaked, number + 1)
                if phase == "max":
                    nc.vector.tensor_reduce(top[:, :], scores, AX.X, ALU.max).then_inc(f_top, 1)
                    dve.wait_ge(f_top, number + 1)
                    nc.vector.tensor_tensor(far_max[:, bass.ds(i, 1)], top[:, :], far_max[:, bass.ds(i, 1)], ALU.max
                                            ).then_inc(f_done, 1)
                    dve.wait_ge(f_done, number + 1)
                    return
                nc.vector.tensor_scalar(neg_max[:, :], far_max[:, bass.ds(i, 1)], -1.0, None, ALU.mult).then_inc(f_neg, 1)
                if phase in ("first sum", "sum"):
                    dve.wait_ge(f_exp, passed + 1)
                    if phase == "sum":
                        nc.vector.tensor_tensor(far_sum[:, bass.ds(i, 1)], chunk_sum[:, 0:1], far_sum[:, bass.ds(i, 1)], ALU.add
                                                ).then_inc(f_sums, 1)
                        dve.wait_ge(f_sums, k * NT + i + 1)
                    nc.vector.tensor_tensor(all_sum[:, bass.ds(i, 1)], chunk_sum[:, 0:1], all_sum[:, bass.ds(i, 1)], ALU.add
                                            ).then_inc(f_done, 1)
                    dve.wait_ge(f_done, number + 1)
                    return
                applied = k * NT + i
                nc.vector.reciprocal(denom[:, 2:3], all_sum[:, bass.ds(i, 1)]).then_inc(f_inverse, 1)
                for c in range(CHUNKS):
                    dve.wait_ge(f_back, CHUNKS * applied + c + 1)
                    nc.vector.tensor_copy(columns(attn, c), attn_ps[c % 2][:, 0:CW]).then_inc(f_attn, 1)
                dve.wait_ge(f_inverse, applied + 1)
                dve.wait_ge(f_aggregated, applied + 1)
                nc.vector.scalar_tensor_tensor(root[:, i, :], sum_ps[0][:, 0:D], denom[:, 2:3], root[:, i, :],
                                               ALU.mult, ALU.add).then_inc(f_done, 1)
                dve.wait_ge(f_done, number + 1)

            with dve.If(nb > 0):
                attention_phases(dve, far_attention_block)

            list_rows(0, 0)
            list_rows(1, 1)
            build_mask(0, 0, ALU.not_equal)

            def attend(i, j, b, last=False):
                use = L * USES[b] + j
                dve.wait_ge(mask_ready[b], use + 1)
                for c in range(CHUNKS + 2):
                    if c < CHUNKS:
                        dve.wait_ge(arrived[b][c], 16 * CHUNK * (use + 1))
                        lower_others(b, CHUNK * c, CHUNK * (c + 1)).then_inc(masked[b], 1)
                    if 1 <= c <= CHUNKS:
                        dve.wait_ge(scored[c - 1], i + 1)
                        leaky(columns(scores, c - 1)).then_inc(leaked, 1)
                    if c >= 2:
                        dve.wait_ge(leaked, CHUNKS * i + c - 1)
                        nc.vector.tensor_reduce(chunk_max[:, c - 2:c - 1], columns(scores, c - 2), AX.X, ALU.max
                                                ).then_inc(max_done, 1)
                dve.wait_ge(max_done, CHUNKS * (i + 1))
                nc.vector.tensor_reduce(top[:, :], chunk_max[:, :], AX.X, ALU.max).then_inc(top_ready, 1)
                dve.wait_ge(top_ready, i + 1)
                nc.vector.tensor_scalar(neg_max[:, :], top[:, :], far_max[:, bass.ds(i, 1)], -1.0, ALU.max, ALU.mult
                                        ).then_inc(neg_max_ready, 1)
                if not last:
                    list_rows(i + 2, b)
                    build_mask(i + 1, 1 - b, ALU.not_equal)
                dve.wait_ge(exp_ready, CHUNKS * (i + 1))
                nc.vector.tensor_reduce(denom[:, 0:1], chunk_sum[:, :], AX.X, ALU.add).then_inc(denom_step, 1)
                dve.wait_ge(denom_step, 3 * i + 1)
                nc.vector.tensor_scalar(denom[:, 1:2], denom[:, 0:1], far_sum[:, bass.ds(i, 1)], None, ALU.add
                                        ).then_inc(denom_step, 1)
                dve.wait_ge(denom_step, 3 * i + 2)
                nc.vector.reciprocal(denom[:, 2:3], denom[:, 1:2]).then_inc(denom_step, 1)
                dve.wait_ge(denom_step, 3 * i + 3)
                dve.wait_ge(aggregated[b][CHUNKS - 1], use + 1)
                dve.wait_ge(out_stored[b], 16 * j)
                nc.vector.scalar_tensor_tensor(z[:, b, :], sum_ps[b][:, 0:D], denom[:, 2:3], root[:, i, :],
                                               ALU.mult, ALU.add).then_inc(out_ready[b], 1)

            with dve.Fori(0, PAIRS) as j:
                attend(2 * j, j, 0)
                attend(2 * j + 1, j, 1)
            attend(NT - 1, PAIRS, 0, last=True)

        @block.scalar
        def _(act):
            def relu_turned(use, b, freed, count):
                act.wait_ge(turned[b], use + 1)
                act.wait_ge(freed, count)
                nc.scalar.activation(xT[:, b, :, :], turn_ps[:, :, :], ACT.Relu).then_inc(xT_ready[b], 1)

            def evacuate(use, b):
                for q in range(R // 2 - 1):
                    act.wait_ge(transformed[b], NB * use + q + 1)
                    if q == 0:
                        act.wait_ge(stored[b], 16 * use)
                    nc.scalar.copy(stage[:, b, 512 * q:512 * (q + 1)], bank[q][:, :]).then_inc(evacuated[q], 1)

            def deviation(t):
                act.wait_ge(mv_ready, t + 1)
                nc.scalar.activation(std[:, :], mean_var[:, 1:2], ACT.Sqrt, bias=eps[:, 0:1]).then_inc(std_ready, 1)

            act.wait_ge(consts_ready, CONSTS)
            deviation(0)
            relu_turned(0, 0, transformed[0], 0)
            with act.Fori(0, PAIRS) as j:
                deviation(2 * j + 1)
                evacuate(j, 0)
                relu_turned(j, 1, transformed[1], NB * j)
                deviation(2 * j + 2)
                evacuate(j, 1)
                relu_turned(j + 1, 0, transformed[0], NB * (j + 1))
            evacuate(PAIRS, 0)

            def to_next_layer(l, j, b):
                use = (l + 1) * USES[b] + j
                relu_turned(use, b, transformed[b], NB * use)
                evacuate(use, b)

            for l in range(L - 1):
                over_tiles(act, lambda i, j, b: to_next_layer(l, j, b))

            def to_attention(i, j, b):
                deviation(NT + i)
                relu_turned(L * USES[b] + j, b, h_ready[b], j)

            over_tiles(act, to_attention)
            for b in range(2):
                act.wait_ge(qk_ready[b], 2 * USES[b])
            load_extra_blocks(act)
            nb = extra(act)

            def add_key(c, i):
                return nc.scalar.activation(columns(scores, c), score_ps[c % 2][:, 0:CW], ACT.Identity,
                                            bias=key[:, bass.ds(i, 1)])

            def far_attention_block(phase, k, i, number, passed):
                for c in range(CHUNKS):
                    settle(act, CHUNKS * number + c + 1)
                    act.wait_ge(f_turned, CHUNKS * number + c + 1)
                    add_key(c, i).then_inc(f_scored, 1)
                if phase != "max":
                    act.wait_ge(f_neg, passed + 1)
                    act.wait_ge(f_scored, CHUNKS * (number + 1))
                    nc.scalar.activation(scores, scores, ACT.Exp, bias=neg_max[:, 0:1],
                                         accum_out=chunk_sum[:, 0:1]).then_inc(f_exp, 1)

            with act.If(nb > 0):
                attention_phases(act, far_attention_block)

            def attend(i, j, b):
                for c in range(CHUNKS):
                    settle(act, CHUNKS * i + c + 1, i)
                    act.wait_ge(score_turned, CHUNKS * i + c + 1)
                    act.wait_ge(attn_turned[c], i)
                    add_key(c, i).then_inc(scored[c], 1)
                act.wait_ge(neg_max_ready, i + 1)
                for c in range(CHUNKS + 2):
                    if c < CHUNKS:
                        nc.scalar.activation(columns(scores, c), columns(scores, c), ACT.Exp, bias=neg_max[:, 0:1],
                                             accum_out=chunk_sum[:, c:c + 1]).then_inc(exp_ready, 1)
                    if c >= 2:
                        act.wait_ge(attn_turned[c - 2], i + 1)
                        nc.scalar.copy(columns(attn, c - 2), attn_ps[c % 2][:, 0:CW]).then_inc(attn_ready[c - 2], 1)

            over_tiles(act, attend)

        @block.tensor
        def _(pe):
            pe.wait_ge(consts_ready, CONSTS)

            def turn(use, b):
                pe.wait_ge(z_ready[b], use + 1)
                for k in range(K):
                    last = nc.tensor.transpose(turn_ps[:, k, :], z[:, b, k * P:(k + 1) * P], ident[:, :])
                last.then_inc(turned[b], 1)

            def transform(step, use, b, banks):
                if banks[0] == 0:
                    pe.wait_ge(xT_ready[b], use + 1)
                for q in banks:
                    pe.wait_ge(evacuated[q], step)
                    width = min(512, (R + 1) * D - 512 * q)
                    for k in range(K):
                        last = nc.tensor.matmul(bank[q][:, 0:width], xT[:, b, k, :],
                                                weights[:, k, 512 * q:512 * q + width],
                                                start=(k == 0), stop=(k == K - 1))
                    last.then_inc(transformed[b], 1)

            AHEAD = list(range(NB - 2))
            REST = list(range(NB - 2, NB))
            turn(0, 0)
            pe.wait_ge(weights_loaded, 16 * (2 * K + 1))
            with pe.Fori(0, PAIRS) as j:
                transform(2 * j, j, 0, AHEAD)
                turn(j, 1)
                transform(2 * j, j, 0, REST)
                transform(2 * j + 1, j, 1, AHEAD)
                turn(j + 1, 0)
                transform(2 * j + 1, j, 1, REST)
            transform(NT - 1, PAIRS, 0, AHEAD + REST)
            load_extra_blocks(pe)
            nb = extra(pe)

            def add_slots(b, lhs, slots, first, last_slot):
                for s in slots:
                    m = nc.tensor.matmul(sum_ps[b][:, 0:D], lhs(s), gathered[:, b, s, 0:D],
                                         start=(s == first), stop=(s == last_slot))
                return m

            def far_conv_block(number):
                pe.wait_ge(far_arrived, 16 * SLOTS * (number + 1))
                pe.wait_ge(far_mask, number + 1)
                add_slots(0, lambda s: masks[:, 0, s, :], range(SLOTS), 0, SLOTS - 1).then_inc(far_aggregated, 1)

            def far_conv(l):
                with pe.If(nb > 0):
                    further(pe, lambda k, i: far_conv_block((l * nb + k) * NT + i))

            def sum_tile(use, b):
                pe.wait_ge(mask_ready[b], use + 1)
                for c in range(CHUNKS):
                    pe.wait_ge(arrived[b][c], 16 * CHUNK * (use + 1))
                    add_slots(b, lambda s: masks[:, b, s, :], range(CHUNK * c, CHUNK * (c + 1)), 0, SLOTS - 1
                              ).then_inc(aggregated[b][c], 1)

            def to_next_layer(l, i, j, b):
                sum_tile(l * USES[b] + j, b)
                use = (l + 1) * USES[b] + j
                turn(use, b)
                transform((l + 1) * NT + i, use, b, AHEAD + REST)

            for l in range(L - 1):
                far_conv(l)
                settle(pe, 16 * (2 * K + 1) * (l + 2))
                pe.wait_ge(weights_loaded, 16 * (2 * K + 1) * (l + 2))
                over_tiles(pe, lambda i, j, b: to_next_layer(l, i, j, b))

            far_conv(L - 1)
            pe.wait_ge(params_loaded, 16 * (5 + K))

            def to_attention(i, j, b):
                sum_tile((L - 1) * USES[b] + j, b)
                use = L * USES[b] + j
                turn(use, b)
                pe.wait_ge(xT_ready[b], use + 1)
                pe.wait_ge(h_biased[b], j)
                for k in range(K):
                    last = nc.tensor.matmul(bank[b][:, 0:D], xT[:, b, k, :], wv_sb[:, k, :],
                                            start=(k == 0), stop=(k == K - 1))
                last.then_inc(h_ready[b], 1)

            over_tiles(pe, to_attention)

            def turn_scores(b, c):
                for s in range(CHUNK):
                    last = nc.tensor.transpose(score_ps[c % 2][:, s * P:(s + 1) * P], masks[:, b, CHUNK * c + s, :],
                                               ident[:, :])
                return last

            def turn_back(c):
                for s in range(CHUNK):
                    at = CW * c + s * P
                    last = nc.tensor.transpose(attn_ps[c % 2][:, s * P:(s + 1) * P], scores[:, at:at + P],
                                               ident[:, :])
                return last

            def attn_slot(s):
                return attn[:, s * P:(s + 1) * P]

            def far_attention_block(phase, k, i, number, passed):
                pe.wait_ge(f_masked, number + 1)
                for c in range(CHUNKS):
                    pe.wait_ge(f_scored, CHUNKS * number + c)
                    turn_scores(0, c).then_inc(f_turned, 1)
                if phase == "apply":
                    pe.wait_ge(f_exp, passed + 1)
                    applied = k * NT + i
                    for c in range(CHUNKS):
                        pe.wait_ge(f_attn, CHUNKS * applied + c)
                        turn_back(c).then_inc(f_back, 1)
                    pe.wait_ge(f_attn, CHUNKS * (applied + 1))
                    add_slots(0, attn_slot, range(SLOTS), 0, SLOTS - 1).then_inc(f_aggregated, 1)

            for b in range(2):
                pe.wait_ge(h_biased[b], USES[b])
            with pe.If(nb > 0):
                attention_phases(pe, far_attention_block)

            def attend(i, j, b):
                use = L * USES[b] + j
                for c in range(CHUNKS):
                    pe.wait_ge(masked[b], CHUNKS * j + c + 1)
                    pe.wait_ge(scored[(c - 2) % CHUNKS], i + 1 if c >= 2 else i)
                    turn_scores(b, c).then_inc(score_turned, 1)
                pe.wait_ge(out_ready[b], j)

                def add_chunk(c):
                    pe.wait_ge(attn_ready[c], i + 1)
                    add_slots(b, attn_slot, range(CHUNK * c, CHUNK * (c + 1)), 0, SLOTS - 1
                              ).then_inc(aggregated[b][c], 1)

                for c in range(CHUNKS):
                    pe.wait_ge(exp_ready, CHUNKS * i + c + 1)
                    pe.wait_ge(attn_ready[(c - 2) % CHUNKS], i + 1 if c >= 2 else i)
                    turn_back(c).then_inc(attn_turned[c], 1)
                    if c:
                        add_chunk(c - 1)
                add_chunk(CHUNKS - 1)

            over_tiles(pe, attend)


_INS = ['x', 'src', 'dst', 'edge_type_8', 'L0_gnn_W_rel', 'L0_gnn_W_root', 'L0_gnn_bias', 'L1_gnn_Wv', 'L1_gnn_bv',
        'L1_gnn_wq', 'L1_gnn_bq', 'L1_gnn_wk', 'L1_gnn_bk']


def kernel(**inputs):
    import concourse.bacc as _bacc
    from concourse.bass_utils import run_bass_kernel_spmd as _run

    nc = _bacc.Bacc("TRN2", target_bir_lowering=False, num_devices=1)
    arrays, args = {}, []
    for name in _INS:
        a = np.ascontiguousarray(inputs[name])
        arrays[f"in_{name}_dram"] = a
        args.append(nc.dram_tensor(f"in_{name}_dram", a.shape, mybir.dt.from_np(a.dtype), kind="ExternalInput").ap())
    args.append(nc.dram_tensor("out_0_dram", inputs['x'].shape, F32, kind="ExternalOutput").ap())
    gnn_program(nc, *args)
    r = _run(nc, [arrays], core_ids=[0])
    return r.results[0]["out_0_dram"]
```

```python
import numpy as np
import concourse.bass as bass
from concourse import mybir
from contextlib import ExitStack

F32 = mybir.dt.float32
I32 = mybir.dt.int32
ALU = mybir.AluOpType
ACT = mybir.ActivationFunctionType
AX = mybir.AxisListType

P = 128
EPS = 1e-5
SLOPE = 0.2
FAR = 1e30
LEAST_MAX = -1e29


def gnn_program(nc, x, src, dst, etype, w_rel, w_root, bias, wv, bv, wq, bq, wk, bk, out):
    N, D = x.shape
    E = src.shape[0]
    L, R = w_rel.shape[0], w_rel.shape[1]
    K = D // P
    NT = (N + P - 1) // P
    LAST = N - (NT - 1) * P
    PAIRS = NT // 2
    assert NT % 2 == 1 and D == K * P and R % 2 == 0
    USES = [PAIRS + 1, PAIRS]
    MEAN = -(-E * P // N)
    CHUNK = 3
    CHUNKS = -(-(MEAN + P) // (P * CHUNK))
    assert CHUNKS % 2 == 0
    SLOTS = CHUNK * CHUNKS
    BLOCK = SLOTS * P
    MAXB = -(-E // BLOCK) + 1
    EROWS = 125
    ECOLS = E // EROWS
    assert E == EROWS * ECOLS
    PADROWS = -(-MAXB * BLOCK // (EROWS * ECOLS))
    EPAD = E * (1 + PADROWS)
    G16 = 16
    GCOLS = -(-E // (P * G16))
    NGROUPS = P * GCOLS
    TROWS = NT * P * R
    HROW = D + 4
    TW = R * D
    CW = CHUNK * P

    tables = [nc.dram_tensor(f"table{l}", (TROWS, D), F32, kind="Internal").ap() for l in range(L)]
    tables_by_node = [t.rearrange("(n r) d -> n (r d)", r=R) for t in tables]
    h_table = nc.dram_tensor("h_table", (NT * P, HROW), F32, kind="Internal").ap()
    features = nc.dram_tensor("features", (NT * P, K * P), F32, kind="Internal").ap()
    code_dram = nc.dram_tensor("code_dram", (EPAD,), I32, kind="Internal").ap()
    dst_dram = nc.dram_tensor("dst_dram", (EPAD,), F32, kind="Internal").ap()

    ctx = ExitStack()
    with ctx:
        def sb(name, shape, dt=F32):
            return ctx.enter_context(nc.sbuf_tensor(name, shape, dt))

        def sem(name):
            return ctx.enter_context(nc.semaphore(name))

        def sems(name, n):
            return [sem(f"{name}{k}") for k in range(n)]

        root = sb("root", [P, NT, D])
        gathered = sb("gathered", [P, 2, SLOTS, HROW])
        masks = sb("masks", [P, 2, SLOTS, P])
        weights = sb("weights", [P, K, (R + 1) * D])
        stage = sb("stage", [P, 2, TW])
        code = sb("code", [P, NT + 1, SLOTS], I32)
        local = sb("local", [P, NT + 1, SLOTS])
        index = [sb(f"index{b}", [P, SLOTS], I32) for b in range(2)]
        x_tile = sb("x_tile", [P, 2, D])
        z = sb("z", [P, 2, D])
        xT = sb("xT", [P, 2, K, P])
        first_T = sb("first_T", [P, 2, K, P])
        first_root = sb("first_root", [P, K, D])
        bias_row = sb("bias_row", [P, D])
        wv_sb = sb("wv_sb", [P, K, D])
        bv_row = sb("bv_row", [P, D])
        wq_row = sb("wq_row", [P, D])
        wk_row = sb("wk_row", [P, D])
        bqk = sb("bqk", [P, 2])
        h_row = sb("h_row", [P, 2, HROW])
        product = sb("product", [P, D])
        summed = sb("summed", [P, D])
        key = sb("key", [P, NT + 1])
        far_max = sb("far_max", [P, NT + 1])
        far_sum = sb("far_sum", [P, NT + 1])
        all_sum = sb("all_sum", [P, NT + 1])
        stats = sb("stats", [P, 6])
        mean_var = sb("mean_var", [P, 2])
        std = sb("std", [P, 1])
        rstd = sb("rstd", [P, 1])
        eps = sb("eps", [P, 1])
        credit = sb("credit", [1, 64])
        chunk_max = sb("chunk_max", [P, CHUNKS])
        top = sb("top", [P, 1])
        neg_max = sb("neg_max", [P, 1])
        chunk_sum = sb("chunk_sum", [P, CHUNKS])
        denom = sb("denom", [P, 3])
        ident = sb("ident", [P, P])
        node_row = sb("node_row", [P, P])
        tile_base = sb("tile_base", [P, NT + 1])
        starts = sb("starts", [1, NT], I32)
        extra_blocks = sb("extra_blocks", [1, 1], I32)
        far_code = sb("far_code", [P, SLOTS], I32)
        far_dst = sb("far_dst", [P, SLOTS])
        far_local = sb("far_local", [P, SLOTS])
        scores = [weights[:, b, 0:SLOTS * P] for b in range(2)]
        attn = stage[:, :, :].rearrange("p b w -> p (b w)")[:, 0:SLOTS * P]
        prep = gathered[:, :, :, :].rearrange("p b s d -> p (b s d)")

        at = [0]

        def room(rows, cols, dt=F32):
            part = prep[0:rows, at[0]:at[0] + cols]
            at[0] += cols
            return part if dt == F32 else part.bitcast(dt)

        src_i, type_i, dst_i = (room(EROWS, ECOLS, I32) for _ in range(3))
        dst_f = room(EROWS, ECOLS)
        at[0] = 0
        groups = room(P, GCOLS * G16)
        least, most = room(P, GCOLS), room(P, GCOLS)
        from_end, from_start = room(P, GCOLS), room(P, GCOLS)
        last_node = room(P, NT)
        meets = room(P, NT * GCOLS).rearrange("p (t g) -> p t g", g=GCOLS)
        other = room(P, NT * GCOLS).rearrange("p (t g) -> p t g", g=GCOLS)
        ends, over_all = room(P, 2 * NT), room(P, 2 * NT)
        start_f, length, top_length = room(1, NT), room(1, NT), room(1, 1)
        block_edges, over = room(1, 64), room(1, 64)
        assert MAXB <= 64 and at[0] <= 2 * SLOTS * HROW
        BOUNDS_STEPS = 10
        SOME = 9
        BESIDE = 0
        MIDDLE = 5
        CREDIT = 1
        CONSTS = 12

        sum_ps = [ctx.enter_context(nc.psum_tensor(f"sum_ps{b}", [P, 512], F32)) for b in range(2)]
        turn_ps = ctx.enter_context(nc.psum_tensor("turn_ps", [P, K, P], F32))
        NB = R // 2 + 1
        bank = [ctx.enter_context(nc.psum_tensor(f"bank{q}", [P, 512], F32)) for q in range(NB)]
        score_ps, attn_ps = bank[0:2], bank[2:4]

        consts_ready = sem("consts_ready")
        prep_step = sem("prep_step")
        prep_dma = sem("prep_dma")
        groups_loaded, numbers_ready = sem("groups_loaded"), sem("numbers_ready")
        bounds_step = sem("bounds_step")
        ends_reduced = sem("ends_reduced")
        starts_ready = sem("starts_ready")
        blocks_loaded = sem("blocks_loaded")
        blocks_local = sem("blocks_local")
        params_loaded = sem("params_loaded")
        weights_loaded = sem("weights_loaded")
        x_first, x_some, x_rest = sem("x_first"), sem("x_some"), sem("x_rest")
        x_loaded = sems("x_loaded", 2)
        stats_ready, mv_ready, rstd_ready = sem("stats_ready"), sem("mv_ready"), sem("rstd_ready")
        std_ready = sem("std_ready")
        z_ready = sems("z_ready", 2)
        turned = sems("turned", 2)
        xT_ready = sems("xT_ready", 2)
        transformed = sems("transformed", 2)
        evacuated = sems("evacuated", NB)
        stored = sems("stored", 2)
        features_stored, features_loaded = sems("features_stored", 2), sems("features_loaded", 2)
        index_ready = sems("index_ready", 2)
        arrived = [sems(f"arrived{b}_", CHUNKS) for b in range(2)]
        mask_ready = sems("mask_ready", 2)
        aggregated = [sems(f"aggregated{b}_", CHUNKS) for b in range(2)]
        summed_ready, residual_ready = sem("summed_ready"), sem("residual_ready")
        h_ready = sems("h_ready", 2)
        h_biased = sems("h_biased", 2)
        dot_ready = sem("dot_ready")
        qk_ready = sems("qk_ready", 2)
        h_stored = sems("h_stored", 2)
        code_shifted = sem("code_shifted")
        others_ready = sems("others_ready", 2)
        masked = sems("masked", 2)
        score_turned = sem("score_turned")
        scored = sems("scored", CHUNKS)
        leaked = sem("leaked")
        max_done = sem("max_done")
        top_ready = sem("top_ready")
        neg_max_ready = sem("neg_max_ready")
        exp_ready = sem("exp_ready")
        attn_turned = sems("attn_turned", CHUNKS)
        attn_ready = sems("attn_ready", CHUNKS)
        denom_step = sem("denom_step")
        out_ready = sems("out_ready", 2)
        out_stored = sems("out_stored", 2)
        far_loaded, far_index, far_arrived, far_localised = (
            sem("far_loaded"), sem("far_index"), sem("far_arrived"), sem("far_localised"))
        far_mask, far_aggregated, far_done = sem("far_mask"), sem("far_aggregated"), sem("far_done")
        f_loaded, f_index, f_arrived, f_localised = (
            sem("f_loaded"), sem("f_index"), sem("f_arrived"), sem("f_localised"))
        f_mask, f_masked, f_turned, f_scored, f_done = (
            sem("f_mask"), sem("f_masked"), sem("f_turned"), sem("f_scored"), sem("f_done"))
        f_top, f_neg, f_exp, f_inverse = sem("f_top"), sem("f_neg"), sem("f_exp"), sem("f_inverse")
        f_back, f_attn, f_aggregated = sem("f_back"), sem("f_attn"), sem("f_aggregated")
        f_sums, f_leaked = sem("f_sums"), sem("f_leaked")

        def settle(eng, *values):
            for value in values:
                if not isinstance(value, int):
                    eng.lower_val(value)
            eng.wait_ge(consts_ready, CONSTS)

        def over_tiles(eng, body):
            with eng.Fori(0, PAIRS) as j:
                body(2 * j, j, 0)
                body(2 * j + 1, j, 1)
            body(NT - 1, PAIRS, 0)

        def slot_columns(t, b, c):
            return t[:, b, CHUNK * c:CHUNK * (c + 1), :]

        def columns(t, c):
            return t[:, CW * c:CW * (c + 1)]

        loaded_extra = {}

        def load_extra_blocks(eng):
            eng.wait_ge(blocks_local, 1)
            loaded_extra[eng.engine] = eng.value_load(extra_blocks[0:1, 0:1], min_val=0, max_val=MAXB)

        def extra(eng):
            return loaded_extra[eng.engine]

        def further(eng, body):
            with eng.Fori(0, extra(eng)) as k:
                with eng.Fori(0, NT) as i:
                    body(k, i)

        def attention_phases(eng, body):
            n = extra(eng)
            with eng.Fori(0, NT) as i:
                body("max", -1, i, i, 0)
            further(eng, lambda k, i: body("max", k, i, (1 + k) * NT + i, 0))
            with eng.Fori(0, NT) as i:
                body("first sum", -1, i, (1 + n) * NT + i, i)
            further(eng, lambda k, i: body("sum", k, i, (2 + n + k) * NT + i, (1 + k) * NT + i))
            further(eng, lambda k, i: body("apply", k, i, (2 + n + n + k) * NT + i, (1 + n + k) * NT + i))

        block = ctx.enter_context(nc.Block())

        @block.gpsimd
        def _(pool):
            pool.iota(node_row[:, :], [[1, P]], base=0, channel_multiplier=0,
                      allow_small_or_imprecise_dtypes=True).then_inc(consts_ready, 1)
            pool.iota(tile_base[:, :], [[P, NT + 1]], base=0, channel_multiplier=0,
                      allow_small_or_imprecise_dtypes=True).then_inc(consts_ready, 1)
            pool.memset(ident[:, :], 0.0).then_inc(prep_step, 1)
            steps = [1]

            def step(instruction):
                steps[0] += 1
                instruction.then_inc(prep_step, 1)
                pool.wait_ge(prep_step, steps[0])

            pool.wait_ge(prep_step, 1)
            pool.affine_select(out=ident[:, :], in_=ident[:, :], compare_op=ALU.not_equal, fill=1.0, base=0,
                               pattern=[[-1, P]], channel_multiplier=1).then_inc(consts_ready, 1)
            pool.memset(far_max[:, :], LEAST_MAX).then_inc(consts_ready, 1)
            pool.memset(far_sum[:, :], 1e-30).then_inc(consts_ready, 1)
            pool.memset(eps[:, :], EPS).then_inc(consts_ready, 1)
            pool.memset(all_sum[:, :], 1e-30).then_inc(consts_ready, 1)
            pool.memset(root[:, NT - 1, :], 0.0).then_inc(consts_ready, 1)
            pool.memset(h_row[:, :, :], 0.0).then_inc(consts_ready, 1)
            pool.memset(code[:, NT, :], 0).then_inc(consts_ready, 1)
            pool.memset(local[:, NT, :], 0.0).then_inc(consts_ready, 1)
            pool.memset(index[1][:, :], 0).then_inc(consts_ready, 1)

            for to, of in ((src_i, src), (type_i, etype), (dst_i, dst)):
                pool.dma_start(to, of.rearrange("(p c) -> p c", p=EROWS)).then_inc(prep_dma, 16)
            pool.wait_ge(prep_dma, 48)
            step(pool.tensor_copy(dst_f, dst_i))
            step(pool.tensor_scalar(src_i, src_i, float(R), None, ALU.mult))
            step(pool.tensor_tensor(src_i, src_i, type_i, ALU.add))
            pool.dma_start(dst_dram[0:E].rearrange("(p c) -> p c", p=EROWS), dst_f).then_inc(prep_dma, 16)
            pool.dma_start(code_dram[0:E].rearrange("(p c) -> p c", p=EROWS), src_i).then_inc(prep_dma, 16)
            step(pool.memset(type_i, 0))
            step(pool.memset(dst_i.bitcast(F32), 1e6))
            for k in range(1, 1 + PADROWS):
                pool.dma_start(code_dram[k * E:(k + 1) * E].rearrange("(p c) -> p c", p=EROWS),
                               type_i).then_inc(prep_dma, 16)
                pool.dma_start(dst_dram[k * E:(k + 1) * E].rearrange("(p c) -> p c", p=EROWS),
                               dst_i.bitcast(F32)).then_inc(prep_dma, 16)
            done = 48 + 32 + 32 * PADROWS
            pool.wait_ge(prep_dma, done)

            pool.dma_start(groups, dst_dram[0:NGROUPS * G16].rearrange("(p c) -> p c", p=P)).then_inc(groups_loaded, 16)
            step(pool.iota(from_end, [[-1, GCOLS]], base=NGROUPS, channel_multiplier=-GCOLS,
                           allow_small_or_imprecise_dtypes=True))
            step(pool.iota(from_start, [[1, GCOLS]], base=1, channel_multiplier=GCOLS,
                           allow_small_or_imprecise_dtypes=True))
            pool.iota(block_edges, [[BLOCK, 64]], base=BLOCK, channel_multiplier=0,
                      allow_small_or_imprecise_dtypes=True).then_inc(numbers_ready, 1)
            pool.wait_ge(bounds_step, BOUNDS_STEPS)
            pool.partition_all_reduce(over_all, ends, P, bass.bass_isa.ReduceOp.max).then_inc(ends_reduced, 1)
            pool.wait_ge(starts_ready, 2)

            with pool.Fori(0, NT) as i:
                start = pool.value_load(starts[0:1, bass.ds(i, 1)], min_val=0, max_val=E)
                pool.dma_start(code[:, i, :], code_dram[bass.ds(start, BLOCK)].rearrange("(p s) -> p s", p=P)
                               ).then_inc(blocks_loaded, 16)
                pool.dma_start(local[:, i, :], dst_dram[bass.ds(start, BLOCK)].rearrange("(p s) -> p s", p=P)
                               ).then_inc(blocks_loaded, 16)
            pool.wait_ge(blocks_loaded, 32 * NT)
            pool.tensor_tensor(local[:, 0:NT, :], local[:, 0:NT, :],
                               tile_base[:, 0:NT].unsqueeze(2).to_broadcast([P, NT, SLOTS]), ALU.subtract
                               ).then_inc(blocks_local, 1)
            load_extra_blocks(pool)

            def gather_tile(l, j, b, table, width):
                use = l * USES[b] + j
                settle(pool, l * (PAIRS + 1) + j + 1, CREDIT + use)
                pool.wait_ge(index_ready[b], l * (PAIRS + 1) + j + 1)
                for c in range(CHUNKS):
                    settle(pool, CREDIT + use)
                    pool.wait_ge(aggregated[b][c], CREDIT + use)
                    for s in range(CHUNK * c, CHUNK * (c + 1)):
                        pool.indirect_dma_start(
                            gathered[:, b, s, 0:width], None, table,
                            bass.IndirectOffsetOnAxis(ap=index[b][:, s:s + 1], axis=0)).then_inc(arrived[b][c], 16)

            def gather_pass(l, table, width):
                over_tiles(pool, lambda i, j, b: gather_tile(l, j, b, table, width))

            def wait_tables(l):
                settle(pool, *(16 * CREDIT + 16 * USES[b] * (l + 1) for b in range(2)))
                for b in range(2):
                    pool.wait_ge(stored[b], 16 * CREDIT + 16 * USES[b] * (l + 1))

            def far_gather(x_done, wait_index, arrives, table, width):
                settle(pool, x_done + 1)
                pool.wait_ge(wait_index, x_done + 1)
                for s in range(SLOTS):
                    pool.indirect_dma_start(
                        gathered[:, 0, s, 0:width], None, table,
                        bass.IndirectOffsetOnAxis(ap=index[0][:, s:s + 1], axis=0)).then_inc(arrives, 16)

            def conv_layer(l):
                wait_tables(l)
                nb = extra(pool)
                with pool.If(nb > 0):
                    further(pool, lambda k, i: far_gather((l * nb + k) * NT + i, far_index, far_arrived,
                                                          tables[l], D))
                    pool.wait_ge(far_done, CREDIT + (l + 1) * nb * NT)
                gather_pass(l, tables[l], D)

            for l in range(L):
                conv_layer(l)

            for b in range(2):
                pool.wait_ge(h_stored[b], 16 * CREDIT + 16 * USES[b])
            nb = extra(pool)
            with pool.If(nb > 0):
                attention_phases(pool, lambda phase, k, i, number, passed: far_gather(
                    number, f_index, f_arrived, h_table, HROW))
                pool.wait_ge(f_done, CREDIT + (2 + nb + nb + nb) * NT)
            gather_pass(L, h_table, HROW)

        @block.sync
        def _(sp):
            def load_weights(l):
                for k in range(K):
                    sp.dma_start(weights[:, k, 0:R * D].rearrange("p (r e) -> p r e", r=R),
                                 w_rel[l, :, k * P:(k + 1) * P, :].rearrange("r p e -> p r e")
                                 ).then_inc(weights_loaded, 16)
                    to = weights[:, k, R * D:(R + 1) * D] if l else first_root[:, k, :]
                    sp.dma_start(to, w_root[l, k * P:(k + 1) * P, :]).then_inc(weights_loaded, 16)
                sp.dma_start(bias_row[:, :], bias[l:l + 1, :].to_broadcast([P, D])).then_inc(weights_loaded, 16)

            def load_x(i, use, b, last=False):
                rows = LAST if last else P
                sp.wait_ge(z_ready[b], CREDIT + use)
                base = (NT - 1) * P if last else i * P
                sp.dma_start(x_tile[0:rows, b, :], x[bass.ds(base, rows), :]).then_inc(x_loaded[b], 16)

            def store_table(l, i, use, b):
                for q in range(R // 2):
                    sp.wait_ge(evacuated[q], CREDIT + NT * l + i + 1)
                sp.dma_start(tables_by_node[l][bass.ds(i * P, P), :], stage[:, b, :]
                             ).then_inc(stored[b], 16)

            def load_start(first, end, arrives):
                sp.dma_start(root[:, first:end, :], x[first * P:end * P, :].rearrange("(n p) d -> p n d", p=P)
                             ).then_inc(arrives, 16)

            load_start(0, 1, x_first)
            load_weights(0)
            load_start(1, SOME, x_some)
            load_start(SOME, NT - 1, x_rest)
            sp.wait_ge(consts_ready, CONSTS)
            sp.dma_start(root[0:LAST, NT - 1, :], x[(NT - 1) * P:N, :]).then_inc(x_rest, 16)
            for row, of in ((bv_row, bv), (wq_row, wq), (wk_row, wk)):
                sp.dma_start(row[:, :], of.unsqueeze(0).to_broadcast([P, D])).then_inc(params_loaded, 16)
            for k, of in enumerate((bq, bk)):
                sp.dma_start(bqk[:, k:k + 1], of.unsqueeze(0).to_broadcast([P, 1])).then_inc(params_loaded, 16)
            for k in range(K):
                sp.dma_start(wv_sb[:, k, :], wv[k * P:(k + 1) * P, :]).then_inc(params_loaded, 16)

            def store_features(i, j, b):
                sp.wait_ge(xT_ready[b], j + 1)
                sp.dma_start(features[bass.ds(i * P, P), :], xT[:, b, :, :].rearrange("p k n -> p (k n)")
                             ).then_inc(features_stored[b], 16)

            def load_features(i, j, b):
                sp.wait_ge(aggregated[b][CHUNKS - 1], CREDIT + j)
                sp.dma_start(first_T[:, b, :, :].rearrange("p k n -> p (k n)"), features[bass.ds(i * P, P), :]
                             ).then_inc(features_loaded[b], 16)

            def before_layers(i, j, b):
                store_features(i, j, b)
                store_table(0, i, j, b)

            over_tiles(sp, before_layers)
            for b in range(2):
                sp.wait_ge(features_stored[b], 16 * CREDIT + 16 * USES[b])
            load_extra_blocks(sp)
            nb = extra(sp)

            def far_load(number, i, k, done, loads):
                sp.wait_ge(done, CREDIT + number)
                start = sp.value_load(starts[0:1, bass.ds(i, 1)], min_val=0, max_val=E)
                at = start + (k + 1) * BLOCK
                sp.dma_start(far_code[:, :], code_dram[bass.ds(at, BLOCK)].rearrange("(p s) -> p s", p=P)
                             ).then_inc(loads, 16)
                sp.dma_start(far_dst[:, :], dst_dram[bass.ds(at, BLOCK)].rearrange("(p s) -> p s", p=P)
                             ).then_inc(loads, 16)

            def far_conv(l):
                with sp.If(nb > 0):
                    further(sp, lambda k, i: far_load((l * nb + k) * NT + i, i, k, far_done, far_loaded))

            for l in range(L - 1):
                for q in range(NB):
                    sp.wait_ge(evacuated[q], CREDIT + NT * (l + 1))
                load_weights(l + 1)
                far_conv(l)
                if l == 0:
                    load_features(0, 0, 0)
                    with sp.Fori(0, PAIRS) as j:
                        load_features(2 * j + 1, j, 1)
                        store_table(1, 2 * j, USES[0] + j, 0)
                        load_features(2 * j + 2, j + 1, 0)
                        store_table(1, 2 * j + 1, USES[1] + j, 1)
                    store_table(1, NT - 1, USES[0] + PAIRS, 0)
                else:
                    over_tiles(sp, lambda i, j, b: store_table(l + 1, i, (l + 1) * USES[b] + j, b))

            far_conv(L - 1)

            def layer_norm_tile(i, j, b, last=False):
                load_x(i, L * USES[b] + j, b, last)

            def store_h(i, j, b):
                sp.wait_ge(qk_ready[b], 2 * (j + 1))
                sp.dma_start(h_table[bass.ds(i * P, P), :], h_row[:, b, :]).then_inc(h_stored[b], 16)

            layer_norm_tile(0, 0, 0)
            with sp.Fori(0, PAIRS - 1) as j:
                layer_norm_tile(2 * j + 1, j, 1)
                store_h(2 * j, j, 0)
                layer_norm_tile(2 * j + 2, j + 1, 0)
                store_h(2 * j + 1, j, 1)
            layer_norm_tile(NT - 2, PAIRS - 1, 1)
            store_h(NT - 3, PAIRS - 1, 0)
            layer_norm_tile(NT - 1, PAIRS, 0, last=True)
            store_h(NT - 2, PAIRS - 1, 1)
            store_h(NT - 1, PAIRS, 0)

            with sp.If(nb > 0):
                attention_phases(sp, lambda phase, k, i, number, passed: far_load(number, i, k, f_done, f_loaded))

            def store_out(i, j, b, last=False):
                sp.wait_ge(out_ready[b], CREDIT + j + 1)
                rows = LAST if last else P
                base = (NT - 1) * P if last else i * P
                sp.dma_start(out[bass.ds(base, rows), :], z[0:rows, b, :]).then_inc(out_stored[b], 16)

            with sp.Fori(0, PAIRS) as j:
                store_out(2 * j, j, 0)
                store_out(2 * j + 1, j, 1)
            store_out(NT - 1, PAIRS, 0, last=True)
            for b in range(2):
                sp.wait_ge(out_stored[b], 16 * CREDIT + 16 * USES[b])

        @block.vector
        def _(dve):
            by_one = (*z_ready, *turned, *transformed, *h_ready, *evacuated, *h_biased, *scored, *out_ready,
                      *attn_ready, *aggregated[0], *aggregated[1], far_done, f_done, f_scored, f_attn)
            for k, counted in enumerate(by_one):
                nc.vector.memset(credit[:, k:k + 1], 0.0).then_inc(counted, CREDIT)
            for k, counted in enumerate((*stored, *h_stored, *out_stored, *features_stored), len(by_one)):
                nc.vector.memset(credit[:, k:k + 1], 0.0).then_inc(counted, 16 * CREDIT)
            dve.wait_ge(consts_ready, CONSTS)

            def statistics(of, t):
                nc.vector.bn_stats(stats[:, :], of).then_inc(stats_ready, 1)
                settle(dve, t + 1)
                dve.wait_ge(stats_ready, t + 1)
                nc.vector.bn_aggr(mean_var[:, :], stats[:, :]).then_inc(mv_ready, 1)
                dve.wait_ge(std_ready, t + 1)
                nc.vector.reciprocal(rstd[:, :], std[:, :]).then_inc(rstd_ready, 1)
                dve.wait_ge(mv_ready, t + 1)
                dve.wait_ge(rstd_ready, t + 1)

            def normalise(of, use, b):
                dve.wait_ge(turned[b], CREDIT + use)
                nc.vector.tensor_scalar(z[:, b, :], of, mean_var[:, 0:1], rstd[:, 0:1], ALU.subtract, ALU.mult
                                        ).then_inc(z_ready[b], 1)

            def evacuate(i, use, b, first=False):
                q = R // 2 - 1
                dve.wait_ge(transformed[b], CREDIT + NB * use + q + 1)
                dve.wait_ge(stored[b], 16 * CREDIT + 16 * use)
                nc.vector.tensor_copy(stage[:, b, 512 * q:512 * (q + 1)], bank[q][:, :]).then_inc(evacuated[q], 1)
                if first:
                    nc.vector.tensor_copy(root[:, i, :], bias_row[:, :]).then_inc(evacuated[NB - 1], 1)
                    return
                dve.wait_ge(transformed[b], CREDIT + NB * use + NB)
                nc.vector.tensor_tensor(root[:, i, :], bank[NB - 1][:, 0:D], bias_row[:, :], ALU.add
                                        ).then_inc(evacuated[NB - 1], 1)

            def first_norm(i, j, b):
                statistics(root[:, i, :], i)
                normalise(root[:, i, :], j, b)

            bounds = [0]

            def step(instruction):
                bounds[0] += 1
                instruction.then_inc(bounds_step, 1)
                dve.wait_ge(bounds_step, bounds[0])

            full_g = [P, NT, GCOLS]

            def per_group(a):
                return a.unsqueeze(1).to_broadcast(full_g)

            def per_tile(a):
                return a.unsqueeze(2).to_broadcast(full_g)

            def group_ranges():
                dve.wait_ge(groups_loaded, 16)
                dve.wait_ge(numbers_ready, 1)
                grouped = groups.rearrange("p (g e) -> p g e", e=G16)
                step(nc.vector.tensor_reduce(least, grouped, AX.X, ALU.min))
                step(nc.vector.tensor_reduce(most, grouped, AX.X, ALU.max))
                step(nc.vector.tensor_scalar(last_node, tile_base[:, 0:NT], float(P - 1), None, ALU.add))

            def reach_start():
                step(nc.vector.tensor_tensor(meets, per_group(most), per_tile(tile_base[:, 0:NT]), ALU.is_ge))
                step(nc.vector.tensor_tensor(other, per_group(least), per_tile(last_node), ALU.is_le))

            def both():
                step(nc.vector.tensor_tensor(meets, meets, other, ALU.mult))

            def end_of(k, number):
                step(nc.vector.tensor_tensor(other, meets, per_group(number), ALU.mult))
                step(nc.vector.tensor_reduce(ends[:, k * NT:(k + 1) * NT], other, AX.X, ALU.max))

            def block_starts():
                assert bounds[0] == BOUNDS_STEPS
                dve.wait_ge(ends_reduced, 1)
                step(nc.vector.tensor_scalar(start_f, over_all[0:1, 0:NT], -float(G16), float(G16 * NGROUPS),
                                             ALU.mult, ALU.add))
                step(nc.vector.tensor_scalar(start_f, start_f, float(E), None, ALU.min))
                step(nc.vector.scalar_tensor_tensor(length, over_all[0:1, NT:2 * NT], float(G16), start_f,
                                                    ALU.mult, ALU.subtract))
                nc.vector.tensor_copy(starts[:, :], start_f).then_inc(starts_ready, 1)
                step(nc.vector.tensor_reduce(top_length, length, AX.X, ALU.max))
                step(nc.vector.tensor_tensor(over, block_edges, top_length.to_broadcast([1, 64]), ALU.is_lt))
                step(nc.vector.tensor_reduce(top_length, over, AX.X, ALU.add))
                nc.vector.tensor_copy(extra_blocks[:, :], top_length).then_inc(starts_ready, 1)

            def before_layers(first, end):
                with dve.Fori(first, end) as j:
                    first_norm(2 * j + 1, j, 1)
                    evacuate(2 * j, j, 0, first=True)
                    first_norm(2 * j + 2, j + 1, 0)
                    evacuate(2 * j + 1, j, 1, first=True)

            dve.wait_ge(x_first, 16)
            first_norm(0, 0, 0)
            dve.wait_ge(weights_loaded, 16 * (2 * K + 1))
            dve.wait_ge(x_some, 16)
            parts = [group_ranges, reach_start, both, lambda: end_of(0, from_end), lambda: end_of(1, from_start),
                     block_starts]
            before_layers(0, 4)
            dve.wait_ge(x_rest, 32)
            for k, part in enumerate(parts):
                part()
                before_layers(4 + 2 * k, 6 + 2 * k)
            before_layers(4 + 2 * len(parts), PAIRS)
            evacuate(NT - 1, PAIRS, 0, first=True)
            load_extra_blocks(dve)
            nb = extra(dve)

            full = [P, SLOTS, P]

            def list_rows(i, b):
                nc.vector.tensor_copy(index[b][:, :], code[:, i, :]).then_inc(index_ready[b], 1)

            def build_mask(i, b, compare):
                nc.vector.tensor_tensor(masks[:, b, :, :], node_row[:, :].unsqueeze(1).to_broadcast(full),
                                        local[:, i, :].unsqueeze(2).to_broadcast(full), compare
                                        ).then_inc(mask_ready[b], 1)

            def far_conv_block(number, i):
                dve.wait_ge(far_loaded, 32 * (number + 1))
                nc.vector.tensor_copy(index[0][:, :], far_code[:, :]).then_inc(far_index, 1)
                nc.vector.tensor_scalar(far_local[:, :], far_dst[:, :], tile_base[:, bass.ds(i, 1)], None, ALU.subtract
                                        ).then_inc(far_localised, 1)
                dve.wait_ge(far_localised, number + 1)
                nc.vector.tensor_tensor(masks[:, 0, :, :], node_row[:, :].unsqueeze(1).to_broadcast(full),
                                        far_local[:, :].unsqueeze(2).to_broadcast(full), ALU.is_equal
                                        ).then_inc(far_mask, 1)
                dve.wait_ge(far_aggregated, number + 1)
                nc.vector.tensor_tensor(root[:, i, :], sum_ps[0][:, 0:D], root[:, i, :], ALU.add
                                        ).then_inc(far_done, 1)
                dve.wait_ge(far_done, CREDIT + number + 1)

            def conv_head(l):
                settle(dve, CREDIT + NT * (l + 1))
                dve.wait_ge(evacuated[NB - 1], CREDIT + NT * (l + 1))
                with dve.If(nb > 0):
                    further(dve, lambda k, i: far_conv_block((l * nb + k) * NT + i, i))
                list_rows(0, 0)
                list_rows(1, 1)
                build_mask(0, 0, ALU.is_equal)

            def conv_tile(l, i, j, b, last):
                use = l * USES[b] + j
                if not last:
                    build_mask(i + 1, 1 - b, ALU.is_equal)
                dve.wait_ge(aggregated[b][CHUNKS - 1], CREDIT + use + 1)
                if not last:
                    list_rows(i + 2, b)

            def to_next_layer(l, i, j, b, last=False):
                conv_tile(l, i, j, b, last)
                use = (l + 1) * USES[b] + j
                dve.wait_ge(turned[b], CREDIT + use)
                nc.vector.tensor_tensor(z[:, b, :], sum_ps[b][:, 0:D], root[:, i, :], ALU.add
                                        ).then_inc(z_ready[b], 1)
                evacuate(i, use, b)

            for l in range(L - 1):
                conv_head(l)
                settle(dve, 16 * (2 * K + 1) * (l + 2))
                dve.wait_ge(weights_loaded, 16 * (2 * K + 1) * (l + 2))
                with dve.Fori(0, PAIRS) as j:
                    to_next_layer(l, 2 * j, j, 0)
                    to_next_layer(l, 2 * j + 1, j, 1)
                to_next_layer(l, NT - 1, PAIRS, 0, last=True)

            conv_head(L - 1)
            dve.wait_ge(params_loaded, 16 * (5 + K))

            def to_attention(i, j, b, last=False):
                conv_tile(L - 1, i, j, b, last)
                nc.vector.tensor_tensor(summed[:, :], sum_ps[b][:, 0:D], root[:, i, :], ALU.add
                                        ).then_inc(summed_ready, 1)
                dve.wait_ge(summed_ready, i + 1)
                dve.wait_ge(x_loaded[b], 16 * (j + 1))
                nc.vector.scalar_tensor_tensor(root[:, i, :], summed[:, :], 0.0, x_tile[:, b, :], ALU.max, ALU.add
                                               ).then_inc(residual_ready, 1)
                settle(dve, i + 1)
                dve.wait_ge(residual_ready, i + 1)
                statistics(root[:, i, :], NT + i)
                normalise(root[:, i, :], L * USES[b] + j, b)
                dve.wait_ge(h_ready[b], CREDIT + j + 1)
                dve.wait_ge(h_stored[b], 16 * CREDIT + 16 * j)
                nc.vector.tensor_tensor(h_row[:, b, 0:D], bank[b][:, 0:D], bv_row[:, :], ALU.add
                                        ).then_inc(h_biased[b], 1)
                dve.wait_ge(h_biased[b], CREDIT + j + 1)
                for k, row in enumerate((wq_row, wk_row)):
                    nc.vector.scalar_tensor_tensor(product[:, :], h_row[:, b, 0:D], 1.0, row[:, :], ALU.mult, ALU.mult,
                                                   accum_out=denom[:, k:k + 1]).then_inc(dot_ready, 1)
                    dve.wait_ge(dot_ready, 2 * i + k + 1)
                nc.vector.tensor_scalar(h_row[:, b, D:D + 1], denom[:, 0:1], bqk[:, 0:1], None, ALU.add
                                        ).then_inc(qk_ready[b], 1)
                nc.vector.tensor_scalar(key[:, bass.ds(i, 1)], denom[:, 1:2], bqk[:, 1:2], None, ALU.add
                                        ).then_inc(qk_ready[b], 1)

            with dve.Fori(0, PAIRS) as j:
                to_attention(2 * j, j, 0)
                to_attention(2 * j + 1, j, 1)
            to_attention(NT - 1, PAIRS, 0, last=True)

            for b in range(2):
                dve.wait_ge(turned[b], CREDIT + (L + 1) * USES[b])
            nc.vector.tensor_scalar(code[:, :, :], code[:, :, :], R.bit_length() - 1, None, ALU.arith_shift_right
                                    ).then_inc(code_shifted, 1)
            dve.wait_ge(code_shifted, 1)

            def lower_others(b, s0, s1):
                return nc.vector.scalar_tensor_tensor(
                    masks[:, b, s0:s1, :], masks[:, b, s0:s1, :], -FAR,
                    gathered[:, b, s0:s1, D:D + 1].to_broadcast([P, s1 - s0, P]), ALU.mult, ALU.add)

            def leaky(part):
                return nc.vector.scalar_tensor_tensor(part, part, SLOPE, part, ALU.mult, ALU.max)

            def far_attention_block(phase, k, i, number, passed):
                dve.wait_ge(f_loaded, 32 * (number + 1))
                nc.vector.tensor_scalar(index[0][:, :], far_code[:, :], R.bit_length() - 1, None,
                                        ALU.arith_shift_right).then_inc(f_index, 1)
                nc.vector.tensor_scalar(far_local[:, :], far_dst[:, :], tile_base[:, bass.ds(i, 1)], None, ALU.subtract
                                        ).then_inc(f_localised, 1)
                dve.wait_ge(f_localised, number + 1)
                nc.vector.tensor_tensor(masks[:, 0, :, :], node_row[:, :].unsqueeze(1).to_broadcast(full),
                                        far_local[:, :].unsqueeze(2).to_broadcast(full), ALU.not_equal
                                        ).then_inc(f_mask, 1)
                dve.wait_ge(f_mask, number + 1)
                dve.wait_ge(f_arrived, 16 * SLOTS * (number + 1))
                lower_others(0, 0, SLOTS).then_inc(f_masked, 1)
                dve.wait_ge(f_scored, CREDIT + CHUNKS * (number + 1))
                leaky(scores[0]).then_inc(f_leaked, 1)
                dve.wait_ge(f_leaked, number + 1)
                if phase == "max":
                    nc.vector.tensor_reduce(top[:, :], scores[0], AX.X, ALU.max).then_inc(f_top, 1)
                    dve.wait_ge(f_top, number + 1)
                    nc.vector.tensor_tensor(far_max[:, bass.ds(i, 1)], top[:, :], far_max[:, bass.ds(i, 1)], ALU.max
                                            ).then_inc(f_done, 1)
                    dve.wait_ge(f_done, CREDIT + number + 1)
                    return
                nc.vector.tensor_scalar(neg_max[:, :], far_max[:, bass.ds(i, 1)], -1.0, None, ALU.mult).then_inc(f_neg, 1)
                if phase in ("first sum", "sum"):
                    dve.wait_ge(f_exp, passed + 1)
                    if phase == "sum":
                        nc.vector.tensor_tensor(far_sum[:, bass.ds(i, 1)], chunk_sum[:, 0:1], far_sum[:, bass.ds(i, 1)], ALU.add
                                                ).then_inc(f_sums, 1)
                        dve.wait_ge(f_sums, k * NT + i + 1)
                    nc.vector.tensor_tensor(all_sum[:, bass.ds(i, 1)], chunk_sum[:, 0:1], all_sum[:, bass.ds(i, 1)], ALU.add
                                            ).then_inc(f_done, 1)
                    dve.wait_ge(f_done, CREDIT + number + 1)
                    return
                applied = k * NT + i
                nc.vector.reciprocal(denom[:, 2:3], all_sum[:, bass.ds(i, 1)]).then_inc(f_inverse, 1)
                for c in range(CHUNKS):
                    dve.wait_ge(f_back, CHUNKS * applied + c + 1)
                    nc.vector.tensor_copy(columns(attn, c), attn_ps[c % 2][:, 0:CW]).then_inc(f_attn, 1)
                dve.wait_ge(f_inverse, applied + 1)
                dve.wait_ge(f_aggregated, applied + 1)
                nc.vector.scalar_tensor_tensor(root[:, i, :], sum_ps[0][:, 0:D], denom[:, 2:3], root[:, i, :],
                                               ALU.mult, ALU.add).then_inc(f_done, 1)
                dve.wait_ge(f_done, CREDIT + number + 1)

            with dve.If(nb > 0):
                attention_phases(dve, far_attention_block)

            list_rows(0, 0)
            list_rows(1, 1)

            def build_chunk(i, b, c):
                part = slice(CHUNK * c, CHUNK * (c + 1))
                shape = [P, CHUNK, P]
                nc.vector.tensor_tensor(masks[:, b, part, :], node_row[:, :].unsqueeze(1).to_broadcast(shape),
                                        local[:, i, part].unsqueeze(2).to_broadcast(shape), ALU.not_equal
                                        ).then_inc(others_ready[b], 1)

            def score_chunk(i, j, b, c):
                dve.wait_ge(others_ready[b], CHUNKS * j + c + 1)
                dve.wait_ge(arrived[b][c], 16 * CHUNK * (L * USES[b] + j + 1))
                lower_others(b, CHUNK * c, CHUNK * (c + 1)).then_inc(masked[b], 1)

            def leaky_chunk(i, b, c):
                dve.wait_ge(scored[c], CREDIT + i + 1)
                leaky(columns(scores[b], c)).then_inc(leaked, 1)

            def max_chunk(i, b, c):
                dve.wait_ge(leaked, CHUNKS * i + c + 1)
                nc.vector.tensor_reduce(chunk_max[:, c:c + 1], columns(scores[b], c), AX.X, ALU.max
                                        ).then_inc(max_done, 1)

            def score_steps(i, j, b, first, end):
                for c in range(first, end):
                    if c < CHUNKS:
                        score_chunk(i, j, b, c)
                    if 2 <= c < CHUNKS + 2:
                        leaky_chunk(i, b, c - 2)
                    if c >= 3:
                        max_chunk(i, b, c - 3)
                    if 2 <= c < CHUNKS + 2:
                        build_chunk(i + 1, 1 - b, c - 2)

            def tile_max(i):
                dve.wait_ge(max_done, CHUNKS * (i + 1))
                nc.vector.tensor_reduce(top[:, :], chunk_max[:, :], AX.X, ALU.max).then_inc(top_ready, 1)
                dve.wait_ge(top_ready, i + 1)
                nc.vector.tensor_scalar(neg_max[:, :], top[:, :], far_max[:, bass.ds(i, 1)], -1.0, ALU.max, ALU.mult
                                        ).then_inc(neg_max_ready, 1)

            def denominator(i):
                dve.wait_ge(exp_ready, CHUNKS * (i + 1))
                nc.vector.tensor_reduce(denom[:, 0:1], chunk_sum[:, :], AX.X, ALU.add).then_inc(denom_step, 1)
                dve.wait_ge(denom_step, 3 * i + 1)
                nc.vector.tensor_scalar(denom[:, 1:2], denom[:, 0:1], far_sum[:, bass.ds(i, 1)], None, ALU.add
                                        ).then_inc(denom_step, 1)
                dve.wait_ge(denom_step, 3 * i + 2)
                nc.vector.reciprocal(denom[:, 2:3], denom[:, 1:2]).then_inc(denom_step, 1)

            def finish(i, j, b):
                dve.wait_ge(denom_step, 3 * i + 3)
                dve.wait_ge(aggregated[b][CHUNKS - 1], CREDIT + L * USES[b] + j + 1)
                dve.wait_ge(out_stored[b], 16 * CREDIT + 16 * j)
                nc.vector.scalar_tensor_tensor(z[:, b, :], sum_ps[b][:, 0:D], denom[:, 2:3], root[:, i, :],
                                               ALU.mult, ALU.add).then_inc(out_ready[b], 1)

            def attend(i, j, b):
                next_j = j if b == 0 else j + 1
                list_rows(i + 2, b)
                score_steps(i + 1, next_j, 1 - b, 0, MIDDLE)
                denominator(i)
                score_steps(i + 1, next_j, 1 - b, MIDDLE, CHUNKS + 3)
                tile_max(i + 1)
                finish(i, j, b)

            for c in range(CHUNKS):
                build_chunk(0, 0, c)
            score_steps(0, 0, 0, 0, CHUNKS + 3)
            tile_max(0)
            with dve.Fori(0, PAIRS) as j:
                attend(2 * j, j, 0)
                attend(2 * j + 1, j, 1)
            denominator(NT - 1)
            finish(NT - 1, PAIRS, 0)

        @block.scalar
        def _(act):
            def relu_turned(use, b, freed, count):
                act.wait_ge(turned[b], CREDIT + use + 1)
                act.wait_ge(freed, CREDIT + count)
                nc.scalar.activation(xT[:, b, :, :], turn_ps[:, :, :], ACT.Relu).then_inc(xT_ready[b], 1)

            def evacuate(use, b):
                for q in range(R // 2 - 1):
                    act.wait_ge(transformed[b], CREDIT + NB * use + q + 1)
                    if q == 0:
                        act.wait_ge(stored[b], 16 * CREDIT + 16 * use)
                    nc.scalar.copy(stage[:, b, 512 * q:512 * (q + 1)], bank[q][:, :]).then_inc(evacuated[q], 1)

            def deviation(t):
                act.wait_ge(mv_ready, t + 1)
                nc.scalar.activation(std[:, :], mean_var[:, 1:2], ACT.Sqrt, bias=eps[:, 0:1]).then_inc(std_ready, 1)

            act.wait_ge(consts_ready, CONSTS)
            deviation(0)
            relu_turned(0, 0, transformed[0], 0)
            with act.Fori(0, PAIRS) as j:
                deviation(2 * j + 1)
                evacuate(j, 0)
                act.wait_ge(features_stored[1], 16 * CREDIT + 16 * j)
                relu_turned(j, 1, transformed[1], NB * j)
                deviation(2 * j + 2)
                evacuate(j, 1)
                act.wait_ge(features_stored[0], 16 * CREDIT + 16 * (j + 1))
                relu_turned(j + 1, 0, transformed[0], NB * (j + 1))
            evacuate(PAIRS, 0)

            for b in range(2):
                act.wait_ge(features_stored[b], 16 * CREDIT + 16 * USES[b])

            def to_next_layer(l, j, b):
                use = (l + 1) * USES[b] + j
                relu_turned(use, b, transformed[b], NB * use)
                evacuate(use, b)

            for l in range(L - 1):
                over_tiles(act, lambda i, j, b: to_next_layer(l, j, b))

            def to_attention(i, j, b):
                deviation(NT + i)
                relu_turned(L * USES[b] + j, b, h_ready[b], j)

            over_tiles(act, to_attention)
            for b in range(2):
                act.wait_ge(qk_ready[b], 2 * USES[b])
            load_extra_blocks(act)
            nb = extra(act)

            def add_key(c, i, b):
                return nc.scalar.activation(columns(scores[b], c), score_ps[c % 2][:, 0:CW], ACT.Identity,
                                            bias=key[:, bass.ds(i, 1)])

            def far_attention_block(phase, k, i, number, passed):
                for c in range(CHUNKS):
                    settle(act, CHUNKS * number + c + 1)
                    act.wait_ge(f_turned, CHUNKS * number + c + 1)
                    add_key(c, i, 0).then_inc(f_scored, 1)
                if phase != "max":
                    act.wait_ge(f_neg, passed + 1)
                    act.wait_ge(f_scored, CREDIT + CHUNKS * (number + 1))
                    nc.scalar.activation(scores[0], scores[0], ACT.Exp, bias=neg_max[:, 0:1],
                                         accum_out=chunk_sum[:, 0:1]).then_inc(f_exp, 1)

            with act.If(nb > 0):
                attention_phases(act, far_attention_block)

            def score_chunk(i, b, c):
                settle(act, CHUNKS * i + c + 1)
                act.wait_ge(score_turned, CHUNKS * i + c + 1)
                add_key(c, i, b).then_inc(scored[c], 1)

            def exponentials(b, c):
                nc.scalar.activation(columns(scores[b], c), columns(scores[b], c), ACT.Exp, bias=neg_max[:, 0:1],
                                     accum_out=chunk_sum[:, c:c + 1]).then_inc(exp_ready, 1)

            def copy_weights(i, c):
                act.wait_ge(attn_turned[c], i + 1)
                nc.scalar.copy(columns(attn, c), attn_ps[c % 2][:, 0:CW]).then_inc(attn_ready[c], 1)

            def attend(i, b, last=False):
                act.wait_ge(neg_max_ready, i + 1)
                for c in range(CHUNKS + 2):
                    if c < CHUNKS:
                        exponentials(b, c)
                    if c >= 2:
                        copy_weights(i, c - 2)
                        if c - 2 >= BESIDE and not last:
                            score_chunk(i + 1, 1 - b, c - 2 - BESIDE)
                if not last:
                    for c in range(CHUNKS - BESIDE, CHUNKS):
                        score_chunk(i + 1, 1 - b, c)

            for c in range(CHUNKS):
                score_chunk(0, 0, c)
            with act.Fori(0, PAIRS) as j:
                attend(2 * j, 0)
                attend(2 * j + 1, 1)
            attend(NT - 1, 0, last=True)

        @block.tensor
        def _(pe):
            pe.wait_ge(consts_ready, CONSTS)

            def turn(use, b):
                pe.wait_ge(z_ready[b], CREDIT + use + 1)
                for k in range(K):
                    last = nc.tensor.transpose(turn_ps[:, k, :], z[:, b, k * P:(k + 1) * P], ident[:, :])
                last.then_inc(turned[b], 1)

            def transform(step, use, b, banks, first=False):
                if banks[0] == 0:
                    pe.wait_ge(xT_ready[b], use + 1)
                for q in banks:
                    pe.wait_ge(evacuated[q], CREDIT + step)
                    width = min(512, (R + 1) * D - 512 * q)
                    for k in range(K):
                        last = nc.tensor.matmul(bank[q][:, 0:width], xT[:, b, k, :],
                                                weights[:, k, 512 * q:512 * q + width],
                                                start=(k == 0), stop=(k == K - 1))
                    last.then_inc(transformed[b], 2 if first and q == NB - 2 else 1)

            AHEAD = list(range(NB - 2))
            REST = list(range(NB - 2, NB))
            FIRST_REST = REST[:-1]
            turn(0, 0)
            pe.wait_ge(weights_loaded, 16 * (2 * K + 1))
            with pe.Fori(0, PAIRS) as j:
                transform(2 * j, j, 0, AHEAD)
                turn(j, 1)
                transform(2 * j, j, 0, FIRST_REST, first=True)
                transform(2 * j + 1, j, 1, AHEAD)
                turn(j + 1, 0)
                transform(2 * j + 1, j, 1, FIRST_REST, first=True)
            transform(NT - 1, PAIRS, 0, AHEAD + FIRST_REST, first=True)
            load_extra_blocks(pe)
            nb = extra(pe)

            def add_slots(b, lhs, slots, first, last_slot):
                for s in slots:
                    m = nc.tensor.matmul(sum_ps[b][:, 0:D], lhs(s), gathered[:, b, s, 0:D],
                                         start=(s == first), stop=(s == last_slot))
                return m

            def far_conv_block(number):
                pe.wait_ge(far_arrived, 16 * SLOTS * (number + 1))
                pe.wait_ge(far_mask, number + 1)
                add_slots(0, lambda s: masks[:, 0, s, :], range(SLOTS), 0, SLOTS - 1).then_inc(far_aggregated, 1)

            def far_conv(l):
                with pe.If(nb > 0):
                    further(pe, lambda k, i: far_conv_block((l * nb + k) * NT + i))

            def sum_tile(use, b, first_use=None):
                pe.wait_ge(mask_ready[b], use + 1)
                if first_use is not None:
                    pe.wait_ge(features_loaded[b], 16 * (first_use + 1))
                    for k in range(K):
                        nc.tensor.matmul(sum_ps[b][:, 0:D], first_T[:, b, k, :], first_root[:, k, :],
                                         start=(k == 0), stop=False)
                first_slot = 0 if first_use is None else None
                for c in range(CHUNKS):
                    pe.wait_ge(arrived[b][c], 16 * CHUNK * (use + 1))
                    add_slots(b, lambda s: masks[:, b, s, :], range(CHUNK * c, CHUNK * (c + 1)), first_slot,
                              SLOTS - 1).then_inc(aggregated[b][c], 1)

            def to_next_layer(l, i, j, b):
                sum_tile(l * USES[b] + j, b, j if l == 0 else None)
                use = (l + 1) * USES[b] + j
                turn(use, b)
                transform((l + 1) * NT + i, use, b, AHEAD + REST)

            for l in range(L - 1):
                far_conv(l)
                settle(pe, 16 * (2 * K + 1) * (l + 2))
                pe.wait_ge(weights_loaded, 16 * (2 * K + 1) * (l + 2))
                over_tiles(pe, lambda i, j, b: to_next_layer(l, i, j, b))

            far_conv(L - 1)
            pe.wait_ge(params_loaded, 16 * (5 + K))

            def to_attention(i, j, b):
                sum_tile((L - 1) * USES[b] + j, b)
                use = L * USES[b] + j
                turn(use, b)
                pe.wait_ge(xT_ready[b], use + 1)
                pe.wait_ge(h_biased[b], CREDIT + j)
                for k in range(K):
                    last = nc.tensor.matmul(bank[b][:, 0:D], xT[:, b, k, :], wv_sb[:, k, :],
                                            start=(k == 0), stop=(k == K - 1))
                last.then_inc(h_ready[b], 1)

            over_tiles(pe, to_attention)

            def turn_scores(b, c):
                for s in range(CHUNK):
                    last = nc.tensor.transpose(score_ps[c % 2][:, s * P:(s + 1) * P], masks[:, b, CHUNK * c + s, :],
                                               ident[:, :])
                return last

            def turn_back(b, c):
                for s in range(CHUNK):
                    at = CW * c + s * P
                    last = nc.tensor.transpose(attn_ps[c % 2][:, s * P:(s + 1) * P], scores[b][:, at:at + P],
                                               ident[:, :])
                return last

            def attn_slot(s):
                return attn[:, s * P:(s + 1) * P]

            def far_attention_block(phase, k, i, number, passed):
                pe.wait_ge(f_masked, number + 1)
                for c in range(CHUNKS):
                    pe.wait_ge(f_scored, CREDIT + CHUNKS * number + c)
                    turn_scores(0, c).then_inc(f_turned, 1)
                if phase == "apply":
                    pe.wait_ge(f_exp, passed + 1)
                    applied = k * NT + i
                    for c in range(CHUNKS):
                        pe.wait_ge(f_attn, CREDIT + CHUNKS * applied + c)
                        turn_back(0, c).then_inc(f_back, 1)
                    pe.wait_ge(f_attn, CREDIT + CHUNKS * (applied + 1))
                    add_slots(0, attn_slot, range(SLOTS), 0, SLOTS - 1).then_inc(f_aggregated, 1)

            for b in range(2):
                pe.wait_ge(h_biased[b], CREDIT + USES[b])
            with pe.If(nb > 0):
                attention_phases(pe, far_attention_block)

            def score_chunk(i, j, b, c):
                pe.wait_ge(masked[b], CHUNKS * j + c + 1)
                pe.wait_ge(scored[(c - 2) % CHUNKS], CREDIT + (i + 1 if c >= 2 else i))
                turn_scores(b, c).then_inc(score_turned, 1)

            def add_chunk(i, b, c):
                pe.wait_ge(attn_ready[c], CREDIT + i + 1)
                add_slots(b, attn_slot, range(CHUNK * c, CHUNK * (c + 1)), 0, SLOTS - 1).then_inc(aggregated[b][c], 1)

            def attend(i, j, b, last=False):
                next_j = j if b == 0 else j + 1
                pe.wait_ge(out_ready[b], CREDIT + j)
                for c in range(CHUNKS + 1):
                    if c < CHUNKS:
                        pe.wait_ge(exp_ready, CHUNKS * i + c + 1)
                        pe.wait_ge(attn_ready[(c - 2) % CHUNKS], CREDIT + (i + 1 if c >= 2 else i))
                        turn_back(b, c).then_inc(attn_turned[c], 1)
                    if c:
                        add_chunk(i, b, c - 1)
                    if BESIDE <= c < CHUNKS and not last:
                        score_chunk(i + 1, next_j, 1 - b, c - BESIDE)
                if not last:
                    for c in range(CHUNKS - BESIDE, CHUNKS):
                        score_chunk(i + 1, next_j, 1 - b, c)

            for c in range(CHUNKS):
                score_chunk(0, 0, 0, c)
            with pe.Fori(0, PAIRS) as j:
                attend(2 * j, j, 0)
                attend(2 * j + 1, j, 1)
            attend(NT - 1, PAIRS, 0, last=True)


_INS = ['x', 'src', 'dst', 'edge_type_8', 'L0_gnn_W_rel', 'L0_gnn_W_root', 'L0_gnn_bias', 'L1_gnn_Wv', 'L1_gnn_bv',
        'L1_gnn_wq', 'L1_gnn_bq', 'L1_gnn_wk', 'L1_gnn_bk']


def kernel(**inputs):
    import concourse.bacc as _bacc
    from concourse.bass_utils import run_bass_kernel_spmd as _run

    nc = _bacc.Bacc("TRN2", target_bir_lowering=False, num_devices=1)
    arrays, args = {}, []
    for name in _INS:
        a = np.ascontiguousarray(inputs[name])
        arrays[f"in_{name}_dram"] = a
        args.append(nc.dram_tensor(f"in_{name}_dram", a.shape, mybir.dt.from_np(a.dtype), kind="ExternalInput").ap())
    args.append(nc.dram_tensor("out_0_dram", inputs['x'].shape, F32, kind="ExternalOutput").ap())
    gnn_program(nc, *args)
    r = _run(nc, [arrays], core_ids=[0])
    return r.results[0]["out_0_dram"]
```
